# Optimizing a Trainium2 kernel written in Bass

```python
import numpy as np
import jax
import jax.numpy as jnp

def _softmax(x, axis=-1):
    return jax.nn.softmax(x, axis=axis)

def _gelu(x):
    return jax.nn.gelu(x, approximate=True)

def _silu(x):
    return jax.nn.silu(x)

def _sigmoid(x):
    return jax.nn.sigmoid(x)

def _layernorm(x, axis=-1, eps=1e-05):
    m = jnp.mean(x, axis=axis, keepdims=True)
    v = jnp.var(x, axis=axis, keepdims=True)
    return (x - m) / jnp.sqrt(v + eps)

def _scatter_add(tgt, idx, src, axis=0):
    return tgt.at[idx].add(src)

def _segment_sum(src, seg, n):
    return jax.ops.segment_sum(src, seg, n)
kernel_name = 'mk_lm_tower_d1_tok_ids1024_r4_c66f20'

def setup_inputs(seed: int=0):
    np.random.seed(seed)
    _w = jnp.asarray

    def _rec_inputs():
        import jax
        import jax.numpy as jnp
        _rk = jax.random.key(seed)
        x = jax.random.randint(jax.random.fold_in(_rk, 1), (8, 512), 0, 31983, jnp.int32)
        return x
    x = _rec_inputs()

    def _L0_tok_setup():
        import jax, jax.numpy as jnp
        import numpy as np
        DEPTH = 8000
        key = jax.random.key(seed)
        k1, k2 = jax.random.split(key)
        inp = jax.random.randint(k1, (64, 32), 0, DEPTH, dtype=jnp.int64 if jax.config.jax_enable_x64 else jnp.int32)
        weight = jax.random.normal(k2, (DEPTH, 256), dtype=jnp.float32)
        return {'input': inp, 'weight': weight}
    _L0_tok_all = _L0_tok_setup()
    _L0_tok_in = {k: v for k, v in _L0_tok_all.items() if k in ('weight',)}
    del _L0_tok_all

    def _L0_attn_setup():
        import jax, jax.numpy as jnp
        import numpy as np
        D_MODEL = 256
        NUM_HEADS = 16
        HEAD_DIM = D_MODEL // NUM_HEADS
        ROPE_THETA = 10000.0

        def apply_rope(x):
            S, d_k = (x.shape[-2], x.shape[-1])
            inv_freq = ROPE_THETA ** (jnp.arange(0, d_k, 2, dtype=jnp.float32) / d_k)
            ang = jnp.arange(S, dtype=jnp.float32)[:, None] / inv_freq[None, :]
            cos, sin = (jnp.cos(ang), jnp.sin(ang))
            xp = x.reshape(x.shape[:-1] + (d_k // 2, 2))
            x0, x1 = (xp[..., 0], xp[..., 1])
            out = jnp.stack([x0 * cos - x1 * sin, x0 * sin + x1 * cos], axis=-1)
            return out.reshape(x.shape)
        key = jax.random.key(seed)
        k1, k2, k3 = jax.random.split(key, 3)
        B, S = (2, 512)
        std = 2.0 / (D_MODEL + 3 * D_MODEL)
        std_o = 2.0 / (D_MODEL + D_MODEL)
        return {'x': jax.random.normal(k1, (B, S, D_MODEL), dtype=jnp.float32), 'W_qkv': jax.random.normal(k2, (3 * D_MODEL, D_MODEL), dtype=jnp.float32) * std, 'W_o': jax.random.normal(k3, (D_MODEL, D_MODEL), dtype=jnp.float32) * std_o}
    _L0_attn_all = _L0_attn_setup()
    _L0_attn_in = {k: v for k, v in _L0_attn_all.items() if k in ('W_qkv', 'W_o')}
    del _L0_attn_all

    def _L0_ffn_setup():
        import jax, jax.numpy as jnp
        import numpy as np
        B, S, H, E = (2, 2048, 256, 8)
        SCALE = 0.5
        key = jax.random.key(seed)
        k1, k2 = jax.random.split(key)
        x = jax.random.normal(k1, (B, S, H), dtype=jnp.float32)
        gate_w = jax.random.normal(k2, (E, H), dtype=jnp.float32) * 0.02
        coeff = SCALE * (1.0 + 0.05 * jnp.arange(E, dtype=jnp.float32))
        expert_w = coeff[:, None, None] * jnp.eye(H, dtype=jnp.float32)
        return {'x': x, 'gate_w': gate_w, 'expert_w': expert_w}
    _L0_ffn_all = _L0_ffn_setup()
    _L0_ffn_in = {k: v for k, v in _L0_ffn_all.items() if k in ('gate_w', 'expert_w')}
    del _L0_ffn_all
    return {'x': x, 'L0_tok_weight': _L0_tok_in['weight'], 'L0_attn_W_qkv': _L0_attn_in['W_qkv'], 'L0_attn_W_o': _L0_attn_in['W_o'], 'L0_ffn_gate_w': _L0_ffn_in['gate_w'], 'L0_ffn_expert_w': _L0_ffn_in['expert_w']}

def reference(x, L0_tok_weight, L0_attn_W_qkv, L0_attn_W_o, L0_ffn_gate_w, L0_ffn_expert_w):
    import jax
    import jax.numpy as jnp

    def _L0_tok_ref(input, weight):
        import jax, jax.numpy as jnp
        import numpy as np
        DEPTH = 8000
        depth = weight.shape[0]
        oh = jax.nn.one_hot(input, depth, dtype=weight.dtype)
        result = jnp.einsum('tbd,de->tbe', oh, weight)
        return result

    def _L0_attn_ref(x, W_qkv, W_o):
        import jax, jax.numpy as jnp
        import numpy as np
        D_MODEL = 256
        NUM_HEADS = 16
        HEAD_DIM = D_MODEL // NUM_HEADS
        ROPE_THETA = 10000.0

        def apply_rope(x):
            S, d_k = (x.shape[-2], x.shape[-1])
            inv_freq = ROPE_THETA ** (jnp.arange(0, d_k, 2, dtype=jnp.float32) / d_k)
            ang = jnp.arange(S, dtype=jnp.float32)[:, None] / inv_freq[None, :]
            cos, sin = (jnp.cos(ang), jnp.sin(ang))
            xp = x.reshape(x.shape[:-1] + (d_k // 2, 2))
            x0, x1 = (xp[..., 0], xp[..., 1])
            out = jnp.stack([x0 * cos - x1 * sin, x0 * sin + x1 * cos], axis=-1)
            return out.reshape(x.shape)
        B, S, d_model = x.shape
        H, d_k = (NUM_HEADS, HEAD_DIM)
        qkv = jnp.einsum('bsi,oi->bso', x, W_qkv)
        Q, K, V = jnp.split(qkv, 3, axis=-1)

        def to_heads(t):
            return t.reshape(B, S, H, d_k).transpose(0, 2, 1, 3)
        Q, K, V = (to_heads(Q), to_heads(K), to_heads(V))
        Q, K = (apply_rope(Q), apply_rope(K))
        scores = jnp.einsum('bhqd,bhkd->bhqk', Q, K) / jnp.sqrt(jnp.float32(d_k))
        causal = jnp.tril(jnp.ones((S, S), dtype=bool))
        scores = jnp.where(causal, scores, -jnp.inf)
        attn = jax.nn.softmax(scores, axis=-1)
        out = jnp.einsum('bhqk,bhkd->bhqd', attn, V)
        out = out.transpose(0, 2, 1, 3).reshape(B, S, d_model)
        return jnp.einsum('bsi,oi->bso', out, W_o)

    def _L0_ffn_ref(x, gate_w, expert_w):
        import jax, jax.numpy as jnp
        import numpy as np
        B, S, H, E = (2, 2048, 256, 8)
        SCALE = 0.5
        scores = jnp.einsum('bsh,eh->bse', x, gate_w)
        chosen = jnp.argmax(scores, axis=-1)
        onehot = jax.nn.one_hot(chosen, gate_w.shape[0], dtype=x.dtype)
        expert_out = jnp.einsum('bsh,efh->bsef', x, expert_w)
        return x + jnp.einsum('bsef,bse->bsf', expert_out, onehot)
    h = _L0_tok_ref(x, L0_tok_weight)
    h = h + _L0_attn_ref(_layernorm(h, axis=-1), L0_attn_W_qkv, L0_attn_W_o)
    h = h + _L0_ffn_ref(_layernorm(h, axis=-1), L0_ffn_gate_w, L0_ffn_expert_w)
    return h

_drawn_inputs = setup_inputs


def setup_inputs(seed=0):
    import zlib

    import numpy as np

    out = dict(_drawn_inputs(seed))
    spreads = {}
    factors = {}
    for name, (base, spread) in spreads.items():
        noise = np.random.default_rng([zlib.crc32(name.encode()), seed]).standard_normal(out[name].shape)
        drawn = base * np.exp(spread * noise) if base else spread * noise
        out[name] = jnp.asarray(drawn.astype(out[name].dtype))
    for name, factor in factors.items():
        out[name] = (out[name] * factor).astype(out[name].dtype)
    return out
```

```python
from contextlib import ExitStack

import numpy as np

import concourse.bass as bass
from concourse import mybir

F32 = mybir.dt.float32
BF16 = mybir.dt.bfloat16
I32 = mybir.dt.int32
U32 = mybir.dt.uint32
ALU = mybir.AluOpType
ACT = mybir.ActivationFunctionType
AX = mybir.AxisListType

P = 128
HEADS = 16
HEAD_DIM = 16
PAIRS = HEAD_DIM // 2
EPS = 1e-5
ROPE_THETA = 10000.0
NEG = -1e30
GROUP = 4
TERMS = [(0, 0), (0, 1), (0, 2), (1, 0), (1, 1), (2, 0)]
TROWS = len(TERMS) * HEAD_DIM
MROWS = 3


class Signal:

    def __init__(self, sem, per, primed=0):
        self.sem, self.per, self.primed = sem, per, primed

    def at(self, b, n):
        return b * self.per + n + self.primed

    def prime(self, engine):
        engine.sem_inc(self.sem, self.primed)


def tower(nc, x, weight, w_qk, w_v, w_o, w_gate, w_exp, rope, ident, identb, mask, out):
    B, S, _ = out.shape
    DEPTH, D = weight.shape
    C = D // P
    T = S // P
    E = w_gate.shape[2]
    G = HEADS // GROUP
    EB = 512 // D
    NEB = E // EB

    U1 = []
    for i in range(T):
        n = min(GROUP, 512 // ((i + 1) * P))
        U1 += [(i, h, n) for h in range(0, GROUP, n)]
    U2 = []
    for j in range(T):
        per_bank = 512 // ((T - j) * P)
        n = min(GROUP, 2 * per_bank)
        U2 += [(j, h, n, per_bank) for h in range(0, GROUP, n)]
    N1, N2 = len(U1), len(U2)
    PRING = 4
    assert (N1 * G) % 2 == 0 and (N2 * G) % PRING == 0

    with ExitStack() as ctx:
        def sb(name, shape, dt=F32):
            return ctx.enter_context(nc.sbuf_tensor(name, shape, dt))

        def signal(name, per, primed=0):
            return Signal(ctx.enter_context(nc.semaphore(name)), per, primed)

        wqk = sb("wqk", [P, C, 4, P])
        wv = sb("wv", [P, C, D])
        wo = sb("wo", [P, C, D])
        wg = sb("wg", [P, C, E])
        we = sb("we", [P, C, E, D])
        trig = sb("trig", [P, 4, S])
        idf = sb("idf", [P, P])
        idb = sb("idb", [P, P], BF16)
        causal = sb("causal", [P, P], BF16)
        rank = sb("rank", [P, E])

        ids = sb("ids", [P, T], I32)
        h = sb("h", [P, T, D])
        stats = sb("stats", [P, T, 6])
        mv = sb("mv", [P, T, 2])
        nv = sb("nv", [P, 4, T])
        xn = sb("xn", [P, T, D])
        xnT = sb("xnT", [P, C, S])
        turn = sb("turn", [P, 2, 4, S])
        qk = sb("qk", [P, 2, 2, S])
        rest = sb("rest", [P, 2, 2, S])
        parts = sb("parts", [P, 3, 2, 2, S], BF16)
        qs = sb("qs", [TROWS + MROWS, HEADS, S], BF16)
        ks = sb("ks", [TROWS + MROWS, HEADS, S], BF16)
        vaug = sb("vaug", [P, T, HEADS, 2 * HEAD_DIM])

        negm = sb("negm", [P, 2, T, GROUP])
        mrest = sb("mrest", [P, 2, T, GROUP])
        mparts = sb("mparts", [P, 2, T, MROWS, GROUP], BF16)
        mrow = sb("mrow", [MROWS * GROUP, 2, S], BF16)
        probs = sb("probs", [P, PRING, 1024])
        oT = sb("oT", [P, 2, S])
        rden = sb("rden", [P, 2, T * GROUP])
        attn = sb("attn", [P, T, D])

        aT = sb("aT", [P, C, S])
        h2 = sb("h2", [P, T, D])
        stats2 = sb("stats2", [P, T, 6])
        mv2 = sb("mv2", [P, T, 2])
        nv2 = sb("nv2", [P, 4, T])
        xn2 = sb("xn2", [P, T, D])
        x2T = sb("x2T", [P, C, S])
        gate = sb("gate", [P, 4, T, E])
        gmax = sb("gmax", [P, 2, T])
        acc = sb("acc", [P, T, D])

        ps = ctx.enter_context(nc.psum_tensor("ps", [P, 8, 512], F32))

        consts = signal("consts", 0)
        s_init = signal("init", 0)
        ids_in = signal("ids_in", 16)
        h_zero = signal("h_zero", 1)
        rows_in = signal("rows_in", 16 * T)
        f_dve = signal("front_dve_step", 2 * T + 1 + 3 * 3 + 1, primed=1)
        xn_rdy = signal("xn_ready", T)
        xt_ps = signal("xT_in_psum", 1)
        xt_rdy = signal("xT_ready", 1)
        qk_ps = signal("qk_in_psum", 4)
        v_ps = signal("v_in_psum", 2)
        v_rdy = signal("v_ready", 2)
        turned = signal("rope_products", 8)
        roped = signal("rope_sums", 4)
        high = signal("high_parts", 2)
        less = signal("rests", 2)
        middle = signal("middle_parts", 2)
        low = signal("low_parts", 2)
        stacked = signal("stacked", 16 * 4 * len(TERMS))
        s1_ps = signal("scores_in_psum", N1 * G)
        s1_max = signal("maxima", N1 * G, primed=1)
        m_step = signal("maxima_split_step", 3 * G)
        m_rdy = signal("maxima_split", G)
        mt_ps = signal("maxT_in_psum", G)
        mt_rdy = signal("maxT_ready", G)
        m_in = signal("max_rows_in", 16 * G)
        s2_ps = signal("scoresT_in_psum", N2 * G)
        exped = signal("exp_done", N2 * G, primed=1)
        masked = signal("probs_masked", N2 * G)
        pv_done = signal("pv_done", N2 * G, primed=1)
        ot_rdy = signal("oT_ready", G, primed=1)
        o_ps = signal("o_in_psum", G)
        rd_rdy = signal("denominators", G)
        at_rdy = signal("attn_ready", G)
        aT_ps = signal("attnT_in_psum", 1)
        aT_rdy = signal("attnT_ready", 1)
        wo_ps = signal("proj_in_psum", 2)
        h2_rdy = signal("h2_ready", 2, primed=1)
        b_dve = signal("back_dve_step", 2 * T + 1 + 3 * 3 + 1)
        xn2_rdy = signal("xn2_ready", T)
        x2_ps = signal("x2T_in_psum", 1)
        x2_rdy = signal("x2T_ready", 1)
        g_ps = signal("gates_in_psum", 1)
        g_step = signal("gate_step", 5)
        base = signal("base_ready", T)
        e_ps = signal("experts_in_psum", T * NEB)
        e_step = signal("expert_sums", T * NEB * EB, primed=1)
        stored = signal("stored", 16, primed=16)
        waited = signal("waited", 0)

        block = ctx.enter_context(nc.Block())
        N_CONST = 10


        def norm(dve, b, src, st, agg, v, dst, step, ready):
            n = [0]

            def link(ins):
                ins.then_inc(step.sem, 1)
                n[0] += 1

            def settle():
                dve.wait_ge(step.sem, step.at(b, n[0]))

            for i in range(T):
                link(nc.vector.bn_stats(st[:, i, :], src[:, i, :]))
            settle()
            dve.sem_inc(waited.sem, 1)
            for i in range(T):
                link(nc.vector.bn_aggr(agg[:, i, :], st[:, i, :]))
            settle()
            nc.vector.tensor_scalar(v[:, 0, :], agg[:, :, 1], EPS, None, ALU.add).then_inc(step.sem, 1)
            n[0] += 1
            settle()
            link(nc.vector.tensor_scalar(v[:, 2, :].bitcast(I32), v[:, 0, :].bitcast(I32), -0.5,
                                         float(0x5F3759DF), ALU.mult, ALU.add))
            settle()
            for k in range(3):
                link(nc.vector.tensor_tensor(v[:, 1, :], v[:, 2, :], v[:, 2, :], ALU.mult))
                settle()
                link(nc.vector.scalar_tensor_tensor(out=v[:, 3, :], in0=v[:, 1, :], scalar=-0.5,
                                                    in1=v[:, 0, :], op0=ALU.mult, op1=ALU.mult))
                settle()
                link(nc.vector.scalar_tensor_tensor(out=v[:, 2, :], in0=v[:, 3, :], scalar=1.5,
                                                    in1=v[:, 2, :], op0=ALU.add, op1=ALU.mult))
                settle()
            assert n[0] == step.per
            for i in range(T):
                nc.vector.tensor_scalar(dst[:, i, :], src[:, i, :], agg[:, i, 0:1], v[:, 2, i:i + 1],
                                        ALU.subtract, ALU.mult).then_inc(ready.sem, 1)

        def p_unit(k, u):
            j, _, n, per_bank = u
            w = (T - j) * P
            return probs[:, k % PRING, 0:n * w].rearrange("p (h w) -> p h w", w=w)

        @block.sync
        def _(sp):
            stored.prime(sp)
            for dst, src in ((wqk, w_qk), (wv, w_v), (wo, w_o), (wg, w_gate), (we, w_exp), (trig, rope),
                             (idf, ident), (idb, identb), (causal, mask[0]), (rank, mask[1])):
                sp.dma_start(dst[:], src).then_inc(consts.sem, 16)
            with sp.Fori(0, B) as b:
                sp.wait_ge(f_dve.sem, f_dve.at(b, 0))
                sp.dma_start(ids[:, :], x[b]).then_inc(ids_in.sem, 16)
                sp.wait_ge(pv_done.sem, pv_done.at(b, 0))
                for part, rdy in ((0, high), (1, middle), (2, low)):
                    for t, dst in ((0, qs), (1, ks)):
                        sp.wait_ge(rdy.sem, rdy.at(b, t + 1))
                        for n, term in enumerate(TERMS):
                            if term[t] == part:
                                for eo in range(2):
                                    r = n * HEAD_DIM + eo * PAIRS
                                    sp.dma_start(dst[r:r + PAIRS, :, :], parts[:, part, t, eo, :])\
                                        .then_inc(stacked.sem, 16)
                for g in range(G):
                    sp.wait_ge(mt_rdy.sem, mt_rdy.at(b, g + 1))
                    sp.dma_start(qs[TROWS:TROWS + MROWS, g * GROUP:(g + 1) * GROUP, :],
                                 mrow[:, g % 2, :]).then_inc(m_in.sem, 16)
                sp.wait_ge(e_step.sem, e_step.at(b, e_step.per))
                sp.dma_start(out[b].rearrange("(i p) d -> p i d", p=P), acc[:, :, :])\
                    .then_inc(stored.sem, 16)
            sp.wait_ge(stored.sem, stored.at(B, 0))

        @block.gpsimd
        def _(pool):
            nc.gpsimd.memset(vaug[:, :, :, :], 1.0).then_inc(s_init.sem, 1)
            zero = pool.to_reg(0.0)
            with pool.Fori(0, B) as b:
                pool.wait_ge(h2_rdy.sem, h2_rdy.at(b, 0))
                pool.sem_inc(waited.sem, 1)
                nc.gpsimd.memset(h[:, :, :], 0.0).then_inc(h_zero.sem, 1)
                pool.wait_ge(h_zero.sem, h_zero.at(b, 1))
                pool.wait_ge(ids_in.sem, ids_in.at(b, 16))
                pool.sem_inc(waited.sem, 1)
                for i in range(T):
                    nc.gpsimd.indirect_dma_start(
                        out=h[:, i, :], out_offset=None, in_=weight,
                        in_offset=bass.IndirectOffsetOnAxis(ap=ids[:, i:i + 1].bitcast(U32), axis=0),
                        bounds_check=DEPTH - 1, oob_is_err=False).then_inc(rows_in.sem, 16)
                for t in range(2):
                    pool.wait_ge(turned.sem, turned.at(b, 4 * t + 2))
                    nc.gpsimd.tensor_tensor(qk[:, t, 0, :], turn[:, t, 0, :], turn[:, t, 1, :],
                                            ALU.subtract).then_inc(roped.sem, 1)
                    pool.wait_ge(turned.sem, turned.at(b, 4 * t + 4))
                    nc.gpsimd.tensor_tensor(qk[:, t, 1, :], turn[:, t, 2, :], turn[:, t, 3, :],
                                            ALU.add).then_inc(roped.sem, 1)
                for g in range(G):
                    for k, u in enumerate(U2):
                        n = g * N2 + k
                        pool.wait_ge(exped.sem, exped.at(b, n + 1))
                        pool.sem_inc(waited.sem, 1)
                        v = p_unit(n, u)[:, :, 0:P]
                        nc.gpsimd.affine_select(out=v, in_=v, compare_op=ALU.is_ge, fill=zero, base=0,
                                                pattern=[[0, u[2]], [1, P]],
                                                channel_multiplier=-1).then_inc(masked.sem, 1)
                pool.wait_ge(stored.sem, stored.at(b, 0))
                for i in range(T):
                    pool.wait_ge(xn2_rdy.sem, xn2_rdy.at(b, i + 1))
                    nc.gpsimd.tensor_tensor(acc[:, i, :], h2[:, i, :], xn2[:, i, :],
                                            ALU.add).then_inc(base.sem, 1)

        @block.scalar
        def _(act):
            exped.prime(act)
            ot_rdy.prime(act)
            with act.Fori(0, B) as b:
                act.wait_ge(xt_ps.sem, xt_ps.at(b, 1))
                nc.scalar.activation(xnT[:, :, :], ps[:, 0:2, :], ACT.Copy).then_inc(xt_rdy.sem, 1)
                act.wait_ge(s_init.sem, 2)
                for k in range(2):
                    act.wait_ge(v_ps.sem, v_ps.at(b, k + 1))
                    nc.scalar.activation(
                        vaug[:, 2 * k:2 * k + 2, :, 0:HEAD_DIM],
                        ps[:, 6 + k, :].rearrange("p (i h d) -> p i h d", i=2, d=HEAD_DIM),
                        ACT.Copy).then_inc(v_rdy.sem, 1)
                for t in range(2):
                    act.wait_ge(roped.sem, roped.at(b, 2 * t + 2))
                    nc.scalar.activation(parts[:, 0, t, :, :], qk[:, t, :, :], ACT.Copy)\
                        .then_inc(high.sem, 1)
                for t in range(2):
                    act.wait_ge(less.sem, less.at(b, t + 1))
                    nc.scalar.activation(parts[:, 1, t, :, :], rest[:, t, :, :], ACT.Copy)\
                        .then_inc(middle.sem, 1)
                for g in range(G):
                    act.wait_ge(mt_ps.sem, mt_ps.at(b, g + 1))
                    if g >= 2:
                        act.wait_ge(m_in.sem, m_in.at(b, 16 * (g - 1)))
                    nc.scalar.activation(mrow[:, g % 2, :],
                                         ps[0:MROWS * GROUP, 7, 0:S // 2].bitcast(BF16),
                                         ACT.Copy).then_inc(mt_rdy.sem, 1)
                    for k, u in enumerate(U2):
                        n = g * N2 + k
                        j, _, nh, per_bank = u
                        act.wait_ge(s2_ps.sem, s2_ps.at(b, n + 1))
                        act.wait_ge(pv_done.sem, pv_done.at(b, max(0, n + 1 - PRING)))
                        bank = 2 + 2 * (n % 2)
                        w = (T - j) * P
                        nb = nh // per_bank
                        src = ps[:, bank:bank + nb, 0:per_bank * w]
                        dst = probs[:, n % PRING, 0:nh * w].rearrange("p (c w) -> p c w", c=nb)
                        nc.scalar.activation(dst, src, ACT.Exp).then_inc(exped.sem, 1)
                    act.wait_ge(pv_done.sem, pv_done.at(b, (g + 1) * N2))
                    nc.scalar.activation(oT[:, g % 2, :], ps[:, 6, :], ACT.Copy).then_inc(ot_rdy.sem, 1)
                act.wait_ge(aT_ps.sem, aT_ps.at(b, 1))
                nc.scalar.activation(aT[:, :, :], ps[:, 0:2, :], ACT.Copy).then_inc(aT_rdy.sem, 1)
                act.wait_ge(x2_ps.sem, x2_ps.at(b, 1))
                nc.scalar.activation(x2T[:, :, :], ps[:, 0:2, :], ACT.Copy).then_inc(x2_rdy.sem, 1)

        @block.vector
        def _(dve):
            for s in (f_dve, h2_rdy, e_step, s1_max):
                s.prime(dve)
            nc.vector.memset(ks[TROWS:TROWS + MROWS, :, :], 1.0).then_inc(s_init.sem, 1)
            dve.wait_ge(consts.sem, 16 * N_CONST)
            with dve.Fori(0, B) as b:
                dve.wait_ge(rows_in.sem, rows_in.at(b, 16 * T))
                norm(dve, b, h, stats, mv, nv, xn, f_dve, xn_rdy)
                for t in range(2):
                    dve.wait_ge(qk_ps.sem, qk_ps.at(b, 2 * t + 2))
                    for n, (eo, f) in enumerate(((0, 0), (1, 1), (0, 1), (1, 0))):
                        nc.vector.tensor_tensor(turn[:, t, n, :], ps[:, 2 + 2 * t + eo, :],
                                                trig[:, 2 * t + f, :], ALU.mult).then_inc(turned.sem, 1)
                for t in range(2):
                    dve.wait_ge(high.sem, high.at(b, t + 1))
                    nc.vector.tensor_tensor(rest[:, t, :, :], qk[:, t, :, :], parts[:, 0, t, :, :],
                                            ALU.subtract).then_inc(less.sem, 1)
                for t in range(2):
                    dve.wait_ge(middle.sem, middle.at(b, t + 1))
                    nc.vector.tensor_tensor(parts[:, 2, t, :, :], rest[:, t, :, :], parts[:, 1, t, :, :],
                                            ALU.subtract).then_inc(low.sem, 1)

                def maxima(g):
                    for k, (i, h0, n) in enumerate(U1):
                        at = g * N1 + k
                        dve.wait_ge(s1_ps.sem, s1_ps.at(b, at + 1))
                        nc.vector.tensor_reduce(
                            negm[:, g % 2, i, h0:h0 + n],
                            ps[:, at % 2, 0:n * (i + 1) * P].rearrange("p (h w) -> p h w", h=n),
                            AX.X, ALU.max, negate=True).then_inc(s1_max.sem, 1)
                    dve.wait_ge(s1_max.sem, s1_max.at(b, (g + 1) * N1))
                    m, r, q = negm[:, g % 2, :, :], mrest[:, g % 2, :, :], mparts[:, g % 2, :, :, :]
                    nc.vector.tensor_copy(q[:, :, 0, :], m).then_inc(m_step.sem, 1)
                    dve.wait_ge(m_step.sem, m_step.at(b, 3 * g + 1))
                    nc.vector.tensor_tensor(r, m, q[:, :, 0, :], ALU.subtract).then_inc(m_step.sem, 1)
                    dve.wait_ge(m_step.sem, m_step.at(b, 3 * g + 2))
                    nc.vector.tensor_copy(q[:, :, 1, :], r).then_inc(m_step.sem, 1)
                    dve.wait_ge(m_step.sem, m_step.at(b, 3 * g + 3))
                    nc.vector.tensor_tensor(q[:, :, 2, :], r, q[:, :, 1, :], ALU.subtract)\
                        .then_inc(m_rdy.sem, 1)

                def divide(g):
                    dve.wait_ge(o_ps.sem, o_ps.at(b, g + 1))
                    o = ps[:, 7, :].rearrange("p (n d) -> p n d", d=2 * HEAD_DIM)
                    r = rden[:, g % 2, :]
                    nc.vector.reciprocal(r, o[:, :, HEAD_DIM]).then_inc(rd_rdy.sem, 1)
                    dve.wait_ge(rd_rdy.sem, rd_rdy.at(b, g + 1))
                    W = GROUP * HEAD_DIM
                    nc.vector.tensor_tensor(
                        attn[:, :, g * W:(g + 1) * W].rearrange("p i (h d) -> p i h d", d=HEAD_DIM),
                        ps[:, 7, :].rearrange("p (i h d) -> p i h d", i=T, d=2 * HEAD_DIM)[:, :, :, 0:HEAD_DIM],
                        r.rearrange("p (i h a) -> p i h a", i=T, a=1).to_broadcast([P, T, GROUP, HEAD_DIM]),
                        ALU.mult).then_inc(at_rdy.sem, 1)

                maxima(0)
                for g in range(G):
                    if g + 1 < G:
                        maxima(g + 1)
                    divide(g)

                for k in range(2):
                    dve.wait_ge(wo_ps.sem, wo_ps.at(b, k + 1))
                    nc.vector.tensor_tensor(h2[:, 2 * k:2 * k + 2, :], h[:, 2 * k:2 * k + 2, :],
                                            ps[:, 6 + k, :].rearrange("p (i d) -> p i d", i=2),
                                            ALU.add).then_inc(h2_rdy.sem, 1)
                dve.wait_ge(h2_rdy.sem, h2_rdy.at(b, 2))
                norm(dve, b, h2, stats2, mv2, nv2, xn2, b_dve, xn2_rdy)
                dve.wait_ge(g_ps.sem, g_ps.at(b, 1))
                sc = ps[:, 6, 0:T * E].rearrange("p (i e) -> p i e", e=E)

                def over(v):
                    return v.unsqueeze(2).to_broadcast([P, T, E])

                nc.vector.tensor_reduce(gmax[:, 0, :], sc, AX.X, ALU.max).then_inc(g_step.sem, 1)
                dve.wait_ge(g_step.sem, g_step.at(b, 1))
                nc.vector.tensor_tensor(gate[:, 0, :, :], sc, over(gmax[:, 0, :]), ALU.is_equal)\
                    .then_inc(g_step.sem, 1)
                dve.wait_ge(g_step.sem, g_step.at(b, 2))
                nc.vector.tensor_tensor(gate[:, 1, :, :], gate[:, 0, :, :],
                                        rank[:, :].unsqueeze(1).to_broadcast([P, T, E]), ALU.mult)\
                    .then_inc(g_step.sem, 1)
                dve.wait_ge(g_step.sem, g_step.at(b, 3))
                nc.vector.tensor_reduce(gmax[:, 1, :], gate[:, 1, :, :], AX.X, ALU.max)\
                    .then_inc(g_step.sem, 1)
                dve.wait_ge(g_step.sem, g_step.at(b, 4))
                nc.vector.tensor_tensor(gate[:, 2, :, :], gate[:, 1, :, :], over(gmax[:, 1, :]),
                                        ALU.is_equal).then_inc(g_step.sem, 1)
                dve.wait_ge(g_step.sem, g_step.at(b, 5))
                for i in range(T):
                    dve.wait_ge(base.sem, base.at(b, i + 1))
                    for k in range(NEB):
                        dve.wait_ge(e_ps.sem, e_ps.at(b, i * NEB + k + 1))
                        for e in range(EB):
                            n = (i * NEB + k) * EB + e
                            if n % E:
                                dve.wait_ge(e_step.sem, e_step.at(b, n))
                            nc.vector.scalar_tensor_tensor(
                                out=acc[:, i, :], in0=ps[:, 2 + k, e * D:(e + 1) * D],
                                scalar=gate[:, 2, i, EB * k + e:EB * k + e + 1], in1=acc[:, i, :],
                                op0=ALU.mult, op1=ALU.add).then_inc(e_step.sem, 1)

        @block.tensor
        def _(pe):
            pv_done.prime(pe)
            pe.wait_ge(consts.sem, 16 * N_CONST)
            pe.wait_ge(s_init.sem, 2)
            with pe.Fori(0, B) as b:
                def transposes(src, ready, count, done):
                    for i in range(T):
                        pe.wait_ge(ready.sem, ready.at(b, count(i)))
                        for c in range(C):
                            mm = pe.transpose(ps[:, c, i * P:(i + 1) * P],
                                              src[:, i, c * P:(c + 1) * P], idf[:, :])
                    mm.then_inc(done.sem, 1)

                transposes(xn, xn_rdy, lambda i: i + 1, xt_ps)
                pe.wait_ge(xt_rdy.sem, xt_rdy.at(b, 1))
                pe.wait_ge(e_step.sem, e_step.at(b, 0))
                for n in range(4):
                    for c in range(C):
                        mm = pe.matmul(ps[:, 2 + n, :], wqk[:, c, n, :], xnT[:, c, :],
                                       start=(c == 0), stop=(c == C - 1))
                    mm.then_inc(qk_ps.sem, 1)
                for i in range(T):
                    for c in range(C):
                        mm = pe.matmul(ps[:, 6 + i // 2, (i % 2) * D:(i % 2 + 1) * D],
                                       xnT[:, c, i * P:(i + 1) * P], wv[:, c, :],
                                       start=(c == 0), stop=(c == C - 1))
                    if i % 2:
                        mm.then_inc(v_ps.sem, 1)
                pe.wait_ge(stacked.sem, stacked.at(b, stacked.per))

                def pass1_unit(g, k):
                    i, h0, n = U1[k]
                    at = g * N1 + k
                    w = (i + 1) * P
                    pe.wait_ge(s1_max.sem, s1_max.at(b, max(0, at - 1)))
                    for x_ in range(n):
                        hd = g * GROUP + h0 + x_
                        pe.matmul(ps[:, at % 2, x_ * w:(x_ + 1) * w], qs[0:TROWS, hd, i * P:(i + 1) * P],
                                  ks[0:TROWS, hd, 0:w], start=True, stop=False)
                        mm = pe.matmul(ps[:, at % 2, (x_ + 1) * w - P:(x_ + 1) * w], idb[:, :],
                                       causal[:, :], start=False, stop=True)
                    mm.then_inc(s1_ps.sem, 1)

                def turn_max(g):
                    pe.wait_ge(m_rdy.sem, m_rdy.at(b, g + 1))
                    if g >= 2:
                        pe.wait_ge(at_rdy.sem, at_rdy.at(b, g - 1))
                    if g == 0:
                        pe.wait_ge(v_rdy.sem, v_rdy.at(b, 2))
                    view = ps[0:MROWS * GROUP, 7, 0:S // 2].bitcast(BF16)
                    for i in range(T):
                        mm = pe.transpose(view[:, i * P:(i + 1) * P],
                                          mparts[:, g % 2, i, :, :].rearrange("p a h -> p (a h)"),
                                          idb[:, :])
                    mm.then_inc(mt_ps.sem, 1)

                def pass2_unit(g, k):
                    j, h0, n, per_bank = U2[k]
                    at = g * N2 + k
                    w = (T - j) * P
                    pe.wait_ge(exped.sem, exped.at(b, max(0, at - 1)))
                    for x_ in range(n):
                        hd = g * GROUP + h0 + x_
                        bank = 2 + 2 * (at % 2) + x_ // per_bank
                        col = (x_ % per_bank) * w
                        mm = pe.matmul(ps[:, bank, col:col + w], ks[:, hd, j * P:(j + 1) * P],
                                       qs[:, hd, j * P:S], start=True, stop=True)
                    mm.then_inc(s2_ps.sem, 1)

                def pv(g, k0, n):
                    for k in range(k0, k0 + n):
                        pe.wait_ge(masked.sem, masked.at(b, g * N2 + k + 1))
                    if k0 == 0:
                        pe.wait_ge(ot_rdy.sem, ot_rdy.at(b, g))
                    for k in range(k0, k0 + n):
                        j, h0, nh, _ = U2[k]
                        pr = p_unit(g * N2 + k, U2[k])
                        for x_ in range(nh):
                            hh = h0 + x_
                            mm = pe.matmul(ps[32 * hh:32 * hh + 32, 6, j * P:S],
                                           vaug[:, j, g * GROUP + hh, :], pr[:, x_, :],
                                           start=(j == 0), stop=(j == T - 1))
                        mm.then_inc(pv_done.sem, 1)

                def turn_out(g):
                    pe.wait_ge(ot_rdy.sem, ot_rdy.at(b, g + 1))
                    pe.wait_ge(mt_rdy.sem, mt_rdy.at(b, min(g + 2, G)))
                    if g >= 1:
                        pe.wait_ge(at_rdy.sem, at_rdy.at(b, g))
                    for i in range(T):
                        mm = pe.transpose(ps[:, 7, i * P:(i + 1) * P], oT[:, g % 2, i * P:(i + 1) * P],
                                          idf[:, :])
                    mm.then_inc(o_ps.sem, 1)

                rows = [[k for k, u in enumerate(U2) if u[0] == j] for j in range(T)]
                for k in range(N1):
                    pass1_unit(0, k)
                turn_max(0)
                for g in range(G):
                    pe.wait_ge(m_in.sem, m_in.at(b, 16 * (g + 1)))
                    ahead = list(range(N1)) if g + 1 < G else []
                    for j in range(T):
                        for k in rows[j]:
                            pass2_unit(g, k)
                            for _ in range(2):
                                if ahead:
                                    pass1_unit(g + 1, ahead.pop(0))
                        if j >= 1:
                            pv(g, rows[j - 1][0], len(rows[j - 1]))
                    while ahead:
                        pass1_unit(g + 1, ahead.pop(0))
                    pv(g, rows[T - 1][0], len(rows[T - 1]))
                    if g + 1 < G:
                        turn_max(g + 1)
                    turn_out(g)

                pe.wait_ge(s1_max.sem, s1_max.at(b, s1_max.per))
                transposes(attn, at_rdy, lambda i: G, aT_ps)
                pe.wait_ge(aT_rdy.sem, aT_rdy.at(b, 1))
                for i in range(T):
                    for c in range(C):
                        mm = pe.matmul(ps[:, 6 + i // 2, (i % 2) * D:(i % 2 + 1) * D],
                                       aT[:, c, i * P:(i + 1) * P], wo[:, c, :],
                                       start=(c == 0), stop=(c == C - 1))
                    if i % 2:
                        mm.then_inc(wo_ps.sem, 1)
                transposes(xn2, xn2_rdy, lambda i: i + 1, x2_ps)
                pe.wait_ge(x2_rdy.sem, x2_rdy.at(b, 1))
                for i in range(T):
                    for c in range(C):
                        mm = pe.matmul(ps[:, 6, i * E:(i + 1) * E], x2T[:, c, i * P:(i + 1) * P],
                                       wg[:, c, :], start=(c == 0), stop=(c == C - 1))
                mm.then_inc(g_ps.sem, 1)
                for i in range(T):
                    for k in range(NEB):
                        n = i * NEB + k
                        if n >= NEB:
                            pe.wait_ge(e_step.sem, e_step.at(b, (n + 1 - NEB) * EB))
                        else:
                            pe.wait_ge(exped.sem, exped.at(b, exped.per))
                        for c in range(C):
                            mm = pe.matmul(ps[:, 2 + k, :], x2T[:, c, i * P:(i + 1) * P],
                                           we[:, c, EB * k:EB * k + EB, :].rearrange("p e d -> p (e d)"),
                                           start=(c == 0), stop=(c == C - 1))
                        mm.then_inc(e_ps.sem, 1)


def kernel(x, L0_tok_weight, L0_attn_W_qkv, L0_attn_W_o, L0_ffn_gate_w, L0_ffn_expert_w):
    import ml_dtypes
    import concourse.bacc as bacc
    from concourse.bass_utils import run_bass_kernel_spmd

    D = L0_tok_weight.shape[1]
    B, S = x.shape
    E = L0_ffn_gate_w.shape[0]
    C = D // P

    def chunks(w_t):
        return np.ascontiguousarray(w_t.reshape(C, P, -1).transpose(1, 0, 2))

    wqkv = np.asarray(L0_attn_W_qkv)
    w_qk = np.stack([wqkv[t * D:(t + 1) * D].reshape(HEADS, PAIRS, 2, D)[:, :, eo].transpose(1, 0, 2).reshape(P, D)
                     for t in range(2) for eo in range(2)])
    w_qk = np.ascontiguousarray(w_qk.transpose(2, 0, 1).reshape(C, P, 4, P).transpose(1, 0, 2, 3))
    w_exp = np.asarray(L0_ffn_expert_w).transpose(2, 0, 1).reshape(C, P, E, D).transpose(1, 0, 2, 3)

    inv = np.float32(ROPE_THETA) ** (np.arange(0, HEAD_DIM, 2, dtype=np.float32) / np.float32(HEAD_DIM))
    ang = np.arange(S, dtype=np.float32)[None, :] / inv[:, None].astype(np.float32)
    cos, sin = (np.repeat(f(ang).astype(np.float32), HEADS, axis=0) for f in (np.cos, np.sin))
    scale = np.float32(HEAD_DIM ** -0.5)
    rope = np.stack([cos * scale, sin * scale, cos, sin], axis=1)
    ident = np.eye(P, dtype=np.float32)
    upper = np.triu(np.full((P, P), NEG, np.float32), 1).astype(ml_dtypes.bfloat16)
    rank = np.tile(np.arange(E, 0, -1, dtype=np.float32), (P, 1))

    arrays = {
        "x": np.ascontiguousarray(np.asarray(x).reshape(B, S // P, P).transpose(0, 2, 1)),
        "weight": np.ascontiguousarray(L0_tok_weight),
        "w_qk": w_qk, "w_v": chunks(wqkv[2 * D:].T), "w_o": chunks(np.asarray(L0_attn_W_o).T),
        "w_gate": chunks(np.asarray(L0_ffn_gate_w).T), "w_exp": np.ascontiguousarray(w_exp),
        "rope": rope, "ident": ident, "identb": ident.astype(ml_dtypes.bfloat16), "mask": upper, "rank": rank,
    }
    nc = bacc.Bacc("TRN2", target_bir_lowering=False, num_devices=1)
    t = {n: nc.dram_tensor(f"in_{n}", a.shape, mybir.dt.from_np(a.dtype), kind="ExternalInput").ap()
         for n, a in arrays.items()}
    out = nc.dram_tensor("out", (B, S, D), F32, kind="ExternalOutput").ap()
    tower(nc, t["x"], t["weight"], t["w_qk"], t["w_v"], t["w_o"], t["w_gate"], t["w_exp"], t["rope"],
          t["ident"], t["identb"], (t["mask"], t["rank"]), out)
    r = run_bass_kernel_spmd(nc, [{f"in_{n}": a for n, a in arrays.items()}], core_ids=[0])
    return r.results[0]["out"]
```

```python
from contextlib import ExitStack

import numpy as np

import concourse.bass as bass
from concourse import mybir

F32 = mybir.dt.float32
BF16 = mybir.dt.bfloat16
I32 = mybir.dt.int32
U32 = mybir.dt.uint32
ALU = mybir.AluOpType
ACT = mybir.ActivationFunctionType
AX = mybir.AxisListType

P = 128
HEADS = 16
HEAD_DIM = 16
PAIRS = HEAD_DIM // 2
EPS = 1e-5
ROPE_THETA = 10000.0
NEG = -1e30
GROUP = 4
TERMS = [(0, 0), (0, 1), (0, 2), (1, 0), (1, 1), (2, 0)]
TROWS = len(TERMS) * HEAD_DIM
MROWS = 3


class Seq:

    def __init__(self, c, q=None):
        self.c, self.q = c, q
        self.index = c if q is None else 2 * q + c
        self.parity = c % 2

    def plus(self, n):
        return Seq(self.c + n, self.q)


class Signal:

    def __init__(self, sem, per, primed=0):
        self.sem, self.per, self.primed = sem, per, primed

    def due(self, s, n):
        return s.q is not None or s.c * self.per + n > 0

    def at(self, s, n):
        value = s.c * self.per + n + self.primed
        assert value > 0, "nothing to wait for, or prime it"
        return value if s.q is None else s.index * self.per + (n + self.primed)


def tower(nc, x, weight, w_qk, w_v, w_o, w_gate, w_exp, rope, ident, identb, mask, tables, out):
    B, S, _ = out.shape
    DEPTH, D = weight.shape
    C = D // P
    T = S // P
    E = w_gate.shape[2]
    G = HEADS // GROUP
    CAP = B * S + P
    W = 2 * D + 4
    NT = B * S // P + E
    RT = 8
    assert NT % RT == 0 and B % 2 == 0 and S == 512

    U1, U2 = [], []
    for i in range(T):
        n = min(GROUP, 512 // ((i + 1) * P))
        U1 += [(i, h, n) for h in range(0, GROUP, n)]
    for j in range(T):
        n = min(GROUP, 512 // ((T - j) * P))
        U2 += [(j, h, n) for h in range(0, GROUP, n)]
    N1, N2 = len(U1), len(U2)
    A1, A2 = N1 * G, N2 * G
    RING = 8
    assert N1 == N2 == 11
    S1B, S2B, PVB, MB = 0, 2, 5, 6

    with ExitStack() as ctx:
        def sb(name, shape, dt=F32):
            return ctx.enter_context(nc.sbuf_tensor(name, shape, dt))

        def signal(name, per, primed=0):
            return Signal(ctx.enter_context(nc.semaphore(name)), per, primed)

        wqk = sb("wqk", [P, C, 4, P])
        wv = sb("wv", [P, C, D])
        wo = sb("wo", [P, C, D])
        wg = sb("wg", [P, C, E])
        we = sb("we", [P, C, E, D])
        trig = sb("trig", [P, 2, S])
        idf = sb("idf", [P, P])
        idb = sb("idb", [P, P], BF16)
        causal = sb("causal", [P, P], BF16)
        rank = sb("rank", [P, E])
        before = sb("before", [P, 2, P], BF16)
        cnt = sb("cnt", [P, E])
        tok = sb("tok", [P, T])
        tab = sb("tab", [1, E + 32 + E * E + 2 * NT])
        ids_all = sb("ids_all", [P, B + 1, T], I32)

        ids = sb("ids", [P, T], I32)
        emb = [sb(f"emb{p}", [P, T, D]) for p in range(2)]
        stats = sb("stats", [P, 2, T, 6])
        mv = sb("mv", [P, 2, T, 2])
        nv = sb("nv", [P, 2, 4, T])
        xn = sb("xn", [P, T, D])
        xnT = sb("xnT", [P, C, S])
        turn = sb("turn", [P, 4, S])
        qk = sb("qk", [P, 2, 2, S])
        parts = sb("parts", [P, 3, 2, 2, S], BF16)
        qs = [sb(f"qs{p}", [TROWS + MROWS, HEADS, S], BF16) for p in range(2)]
        ks = [sb(f"ks{p}", [TROWS + MROWS, HEADS, S], BF16) for p in range(2)]
        VN = T * HEADS * 2 * HEAD_DIM
        vbuf = sb("vbuf", [P, max(2 * VN, RT * W)])
        vaug = [vbuf[:, p * VN:(p + 1) * VN].rearrange("p (i h d) -> p i h d", i=T, h=HEADS)
                for p in range(2)]

        negm = sb("negm", [P, 2, T, GROUP])
        mrest = sb("mrest", [P, 2, T, GROUP])
        mparts = sb("mparts", [P, 2, T, MROWS, GROUP], BF16)
        mrow = sb("mrow", [MROWS * GROUP, 2, S], BF16)
        probs = sb("probs", [P, RING, 512])
        oT = sb("oT", [P, 2, S])
        rden = sb("rden", [P, 2, T * GROUP])
        attn = sb("attn", [P, T, D])

        res = sb("res", [P, T, D])
        bT = sb("bT", [P, C, S])
        h2 = sb("h2", [P, T, D])
        gate = sb("gate", [P, 2, T, E])
        gmax = sb("gmax", [P, 2, T])
        xr = sb("xr", [P, T, W])
        xn2 = xr[:, :, 0:D]
        onehot = sb("onehot", [P, T, E], BF16)
        slot = sb("slot", [P, 2, T, E])
        pos = sb("pos", [P, 2, T])

        cnt_i = sb("cnt_i", [1, E], I32)
        tiles = sb("tiles", [1, 2, NT], I32)
        tw = turn[0:1, :, 0:NT * E]
        tn = qk[0:1, 0, :, :].rearrange("p a s -> p (a s)")[:, 0:8 * NT].rearrange("p (a n) -> p a n", n=NT)
        pad = probs[:, 0:2, :].rearrange("p a s -> p (a s)")[:, 0:W]
        y = probs[:, 4:8, :].rearrange("p a (b d) -> p (a b) d", d=D)
        xin = vbuf[:, 0:RT * W].rearrange("p (u w) -> p u w", w=W)
        xinT = sb("xinT", [P, 2, C, P])

        ps = ctx.enter_context(nc.psum_tensor("ps", [P, 8, 512], F32))

        NORM_STEPS = 2 * T + 2 + 3 * 3
        consts = signal("consts", 0)
        s_init = signal("init", 0)
        ids_cp = signal("ids_copied", 1)
        emb_zero = signal("emb_zero", 1)
        rows_in = signal("rows_in", 16 * T)
        res_in = signal("residual_in", 16)
        n_step = [signal("front_norm_step", NORM_STEPS), signal("back_norm_step", NORM_STEPS, 1)]
        xn_rdy = signal("xn_ready", T)
        xt_ps = signal("xT_in_psum", C)
        xt_rdy = signal("xT_ready", C)
        qk_ps = signal("qk_in_psum", 4)
        v_ps = signal("v_in_psum", 2)
        v_rdy = signal("v_ready", 2)
        turned = signal("rope_products", 8)
        roped = signal("rope_sums", 4)
        high = signal("high_parts", 2)
        less = signal("rests", 2)
        middle = signal("middle_parts", 2)
        low = signal("low_parts", 2)
        stacked = signal("stacked", 16 * 4 * len(TERMS))
        s1_ps = signal("scores_in_psum", A1)
        s1_max = signal("maxima", A1)
        m_step = signal("maxima_split_step", 3 * G)
        m_rdy = signal("maxima_split", G)
        mt_ps = signal("maxT_in_psum", G)
        mt_rdy = signal("maxT_ready", G)
        m_in = [signal(f"max_rows_in{p}", 16 * G // 2) for p in range(2)]
        s2_ps = signal("scoresT_in_psum", A2)
        exped = signal("exp_done", A2)
        masked = signal("probs_masked", A2)
        pv_done = signal("pv_done", A2)
        ot_rdy = signal("oT_ready", G)
        o_ps = signal("o_in_psum", G)
        rd_rdy = signal("denominators", G)
        at_rdy = signal("attn_ready", G)
        aT_ps = signal("attnT_in_psum", C, 1)
        aT_rdy = signal("attnT_ready", C)
        wo_ps = signal("proj_in_psum", 2)
        h2_rdy = signal("h2_ready", 2)
        xn2_rdy = signal("xn2_ready", T)
        x2_ps = signal("x2T_in_psum", C)
        x2_rdy = signal("x2T_ready", C)
        g_ps = signal("gates_in_psum", 1, 1)
        g_step = signal("gate_step", 5)
        base = signal("base_ready", T, 1)
        r_ps = signal("ranks_in_psum", 1)
        r_step = signal("route_step", 6, 1)
        p_rdy = signal("positions_ready", 1)
        routed = signal("rows_routed", 16 * T)
        xr_free = signal("routed_rows_free", 1, 1)
        padded = signal("pads_written", 0)
        t_step = signal("tile_table_step", 0)
        tile_in = [signal(f"tile{u}_in", 16) for u in range(RT)]
        xi_ps = signal("tileT_in_psum", RT)
        xi_rdy = signal("tileT_ready", RT)
        y_ps = signal("y_in_psum", RT)
        y_rdy = signal("y_ready", RT)
        y_out = signal("y_scattered", 16 * RT)
        waited = signal("waited", 0)

        block = ctx.enter_context(nc.Block())
        N_CONST = 15
        N_TSTEP = 15
        N_INIT = 6
        routed_rows = nc.dram_tensor("routed_rows", (E * CAP + P, W), F32, kind="Internal").ap()
        out_rows = out.rearrange("b s d -> (b s) d")


        def schedule(engine, before_first, body, after_last):
            before_first(Seq(-1))
            body(Seq(0), True, False)
            with engine.Fori(0, B // 2 - 1) as q:
                body(Seq(1, q), False, False)
                body(Seq(2, q), False, False)
            body(Seq(B - 1), False, True)
            after_last(Seq(B - 1))

        def p_unit(k, u):
            j, _, n = u
            w = (T - j) * P
            return probs[:, k % RING, 0:n * w].rearrange("p (h w) -> p h w", w=w)

        def misc(s, m):
            return MB + (m + s.parity) % 2

        @block.sync
        def _(sp):
            sp.dma_start(ids_all[:, 0:B, :], x).then_inc(consts.sem, 16)
            for dst, src in ((trig, rope), (idf, ident), (wqk, w_qk), (wv, w_v),
                             (idb, identb), (causal, mask[0]), (wo, w_o), (wg, w_gate), (rank, mask[1]),
                             (before, tables[0]), (cnt, tables[1]), (tok, tables[2]), (tab, tables[3]),
                             (we, w_exp)):
                sp.dma_start(dst[:], src).then_inc(consts.sem, 16)

            def stack(f, part, t):
                part_rdy = (high, middle, low)[part]
                sp.wait_ge(part_rdy.sem, part_rdy.at(f, t + 1))
                dst = (qs, ks)[t][f.parity]
                for n, term in enumerate(TERMS):
                    if term[t] == part:
                        for eo in range(2):
                            r = n * HEAD_DIM + eo * PAIRS
                            sp.dma_start(dst[r:r + PAIRS, :, :], parts[:, part, t, eo, :])\
                                .then_inc(stacked.sem, 16)

            def max_rows(s, g):
                sp.wait_ge(mt_rdy.sem, mt_rdy.at(s, g + 1))
                sp.dma_start(qs[s.parity][TROWS:TROWS + MROWS, g * GROUP:(g + 1) * GROUP, :],
                             mrow[:, g % 2, :]).then_inc(m_in[g % 2].sem, 16)

            def start(s):
                f = s.plus(1)
                for part in range(3):
                    stack(f, part, 0)
                    stack(f, part, 1)
                max_rows(f, 0)

            def body(s, first, last):
                f = s.plus(1)
                max_rows(s, 1)
                if not last:
                    if s2_ps.due(s, 0):
                        sp.wait_ge(s2_ps.sem, s2_ps.at(s, 0))
                    stack(f, 0, 0)
                    stack(f, 0, 1)
                max_rows(s, 2)
                if not last:
                    stack(f, 1, 0)
                    stack(f, 1, 1)
                    stack(f, 2, 0)
                    stack(f, 2, 1)
                if not first:
                    if h2_rdy.due(s, 0):
                        sp.wait_ge(h2_rdy.sem, h2_rdy.at(s, 0))
                sp.wait_ge(rows_in.sem, rows_in.at(s, 16 * T))
                sp.dma_start(res[:, :, :], emb[s.parity][:, :, :]).then_inc(res_in.sem, 16)
                max_rows(s, 3)
                if not last:
                    max_rows(f, 0)

            schedule(sp, start, body, lambda s: None)

            sp.wait_ge(routed.sem, B * routed.per)
            sp.wait_ge(t_step.sem, 2)
            sp.dma_start(routed_rows[E * CAP:E * CAP + P, :], pad).then_inc(padded.sem, 16)
            for e in range(E):
                row = sp.value_load(cnt_i[0:1, e:e + 1], min_val=e * CAP, max_val=(e + 1) * CAP - P)
                sp.dma_start(routed_rows[bass.ds(row, P), :], pad).then_inc(padded.sem, 16)
            sp.wait_ge(padded.sem, 16 * (E + 1))
            sp.wait_ge(t_step.sem, N_TSTEP)

            def load(r, u):
                row = sp.value_load(tiles[0:1, 0, bass.ds(r * RT + u, 1)], min_val=0, max_val=E * CAP)
                sp.dma_start(xin[:, u, :], routed_rows[bass.ds(row, P), :]).then_inc(tile_in[u].sem, 16)

            for u in range(RT):
                load(0, u)
            with sp.Fori(1, NT // RT) as r:
                sp.wait_ge(y_out.sem, r * y_out.per)
                for u in range(RT):
                    load(r, u)
            sp.wait_ge(y_out.sem, NT // RT * y_out.per)

        @block.gpsimd
        def _(pool):
            nc.gpsimd.memset(vaug[0][:, :, :, :], 1.0).then_inc(s_init.sem, 1)
            nc.gpsimd.memset(vaug[1][:, :, :, :], 1.0).then_inc(s_init.sem, 1)
            nc.gpsimd.memset(ids_all[:, B, :], DEPTH).then_inc(s_init.sem, 1)
            for sig in (base, xr_free):
                pool.sem_inc(sig.sem, sig.primed)
            pool.wait_ge(consts.sem, 16 * N_CONST)
            zero = pool.to_reg(0.0)

            def gather_start(n):
                if rows_in.due(n, 0):
                    pool.wait_ge(rows_in.sem, rows_in.at(n, 0))
                pool.sem_inc(waited.sem, 1)
                nc.gpsimd.tensor_copy(ids[:, :], ids_all[:, n.c, :] if n.q is None else
                                      ids_all[:, bass.ds(n.index, 1), :].rearrange("p a i -> p (a i)"))\
                    .then_inc(ids_cp.sem, 1)
                nc.gpsimd.memset(emb[n.parity][:, :, :], 0.0).then_inc(emb_zero.sem, 1)
                pool.wait_ge(ids_cp.sem, ids_cp.at(n, 1))
                pool.wait_ge(emb_zero.sem, emb_zero.at(n, 1))
                pool.sem_inc(waited.sem, 1)

            def gather(n, i):
                nc.gpsimd.indirect_dma_start(
                    out=emb[n.parity][:, i, :], out_offset=None, in_=weight,
                    in_offset=bass.IndirectOffsetOnAxis(ap=ids[:, i:i + 1].bitcast(U32), axis=0),
                    bounds_check=DEPTH - 1, oob_is_err=False).then_inc(rows_in.sem, 16)

            def rope_sum(f, t, eo):
                pool.wait_ge(turned.sem, turned.at(f, 4 * t + 2 * eo + 2))
                if t == 0:
                    if low.due(f, 0):
                        pool.wait_ge(low.sem, low.at(f, 0))
                nc.gpsimd.tensor_tensor(qk[:, t, eo, :], turn[:, 2 * eo, :], turn[:, 2 * eo + 1, :],
                                        ALU.add if eo else ALU.subtract).then_inc(roped.sem, 1)

            def rest(f, t):
                pool.wait_ge(high.sem, high.at(f, t + 1))
                nc.gpsimd.tensor_tensor(qk[:, t, :, :], qk[:, t, :, :], parts[:, 0, t, :, :],
                                        ALU.subtract).then_inc(less.sem, 1)

            def low_part(f, t):
                pool.wait_ge(middle.sem, middle.at(f, t + 1))
                nc.gpsimd.tensor_tensor(parts[:, 2, t, :, :], qk[:, t, :, :], parts[:, 1, t, :, :],
                                        ALU.subtract).then_inc(low.sem, 1)

            def mask_unit(s, g, k):
                n = g * N2 + k
                pool.wait_ge(exped.sem, exped.at(s, n + 1))
                pool.sem_inc(waited.sem, 1)
                v = p_unit(n, U2[k])[:, :, 0:P]
                nc.gpsimd.affine_select(out=v, in_=v, compare_op=ALU.is_ge, fill=zero, base=0,
                                        pattern=[[0, U2[k][2]], [1, P]],
                                        channel_multiplier=-1).then_inc(masked.sem, 1)

            def base_tile(k, i):
                pool.wait_ge(xn2_rdy.sem, xn2_rdy.at(k, i + 1))
                nc.gpsimd.tensor_tensor(xr[:, i, D:2 * D], h2[:, i, :], xn2[:, i, :],
                                        ALU.add).then_inc(base.sem, 1)

            def route(k, i):
                if i == 0:
                    pool.wait_ge(p_rdy.sem, p_rdy.at(k, 1))
                    pool.wait_ge(base.sem, base.at(k, T))
                    pool.sem_inc(waited.sem, 1)
                nc.gpsimd.indirect_dma_start(
                    out=routed_rows, in_=xr[:, i, :], in_offset=None,
                    out_offset=bass.IndirectOffsetOnAxis(ap=pos[:, 1, i:i + 1].bitcast(U32), axis=0),
                    bounds_check=E * CAP - 1, oob_is_err=False).then_inc(routed.sem, 16)

            def start(s):
                f = s.plus(1)
                gather_start(f)
                for i in range(T):
                    gather(f, i)
                for t in range(2):
                    for eo in range(2):
                        rope_sum(f, t, eo)
                for t in range(2):
                    rest(f, t)
                for t in range(2):
                    low_part(f, t)
                gather_start(s.plus(2))
                for i in range(T):
                    gather(s.plus(2), i)

            def body(s, first, last):
                f, k_, n = s.plus(1), s.plus(-1), s.plus(2)
                for g in range(G):
                    for k in range(N2):
                        mask_unit(s, g, k)
                        if not last:
                            if g == 1 and k in (0, 1):
                                rope_sum(f, 0, k)
                            if g == 1 and k in (3, 4):
                                rope_sum(f, 1, k - 3)
                            if g == 1 and k in (6, 9):
                                rest(f, k // 9)
                            if g == 2 and k in (2, 4):
                                low_part(f, k // 4)
                            if g == 3 and k == 3:
                                pool.wait_ge(res_in.sem, res_in.at(s, 16))
                                gather_start(n)
                            if g == 3 and k in (4, 5):
                                gather(n, 2 * k - 8)
                                gather(n, 2 * k - 7)
                        if not first:
                            if g == 2 and k in (7, 8, 9, 10):
                                base_tile(k_, k - 7)
                            if g == 3 and k in (6, 7):
                                route(k_, 2 * k - 12)
                                route(k_, 2 * k - 11)
                            if g == 3 and k == 10:
                                pool.wait_ge(routed.sem, routed.at(k_, 16 * T))
                                pool.sem_inc(xr_free.sem, 1)

            def end(s):
                for i in range(T):
                    base_tile(s, i)
                for i in range(T):
                    route(s, i)

            schedule(pool, start, body, end)
            with pool.Fori(0, NT // RT) as r:
                for u in range(RT):
                    pool.wait_ge(y_rdy.sem, r * y_rdy.per + (u + 1))
                    pool.sem_inc(waited.sem, 1)
                    nc.gpsimd.indirect_dma_start(
                        out=out_rows, in_=y[:, u, :], in_offset=None,
                        out_offset=bass.IndirectOffsetOnAxis(ap=xin[:, u, 2 * D:2 * D + 1].bitcast(U32), axis=0),
                        bounds_check=B * S - 1, oob_is_err=False).then_inc(y_out.sem, 16)

        @block.scalar
        def _(act):
            act.sem_inc(s_init.sem, 1)

            def copy(dst, src, done):
                nc.scalar.activation(dst, src, ACT.Copy).then_inc(done.sem, 1)

            def xT(s, c):
                f = s.plus(1)
                act.wait_ge(xt_ps.sem, xt_ps.at(f, c + 1))
                if v_ps.due(f, 0):
                    act.wait_ge(v_ps.sem, v_ps.at(f, 0))
                copy(xnT[:, c, :], ps[:, misc(s, 1 + c), :], xt_rdy)

            def v_half(s, k):
                f = s.plus(1)
                act.wait_ge(v_ps.sem, v_ps.at(f, k + 1))
                if pv_done.due(s, 0):
                    act.wait_ge(pv_done.sem, pv_done.at(s, 0))
                copy(vaug[f.parity][:, 2 * k:2 * k + 2, :, 0:HEAD_DIM],
                     ps[:, misc(s, 20 + k), :].rearrange("p (i h d) -> p i h d", i=2, d=HEAD_DIM), v_rdy)

            def high_part(f, t):
                act.wait_ge(roped.sem, roped.at(f, 2 * t + 2))
                if stacked.due(f, 0):
                    act.wait_ge(stacked.sem, stacked.at(f, 0))
                copy(parts[:, 0, t, :, :], qk[:, t, :, :], high)

            def middle_part(f, t):
                act.wait_ge(less.sem, less.at(f, t + 1))
                copy(parts[:, 1, t, :, :], qk[:, t, :, :], middle)

            def max_row(s, g, bank):
                act.wait_ge(mt_ps.sem, mt_ps.at(s, g + 1))
                used = m_in[g % 2]
                if used.due(s, 16 * (g // 2)):
                    act.wait_ge(used.sem, used.at(s, 16 * (g // 2)))
                copy(mrow[:, g % 2, :], ps[0:MROWS * GROUP, bank, 0:S // 2].bitcast(BF16), mt_rdy)

            def exp_unit(s, g, k):
                n = g * N2 + k
                j, _, nh = U2[k]
                w = nh * (T - j) * P
                act.wait_ge(s2_ps.sem, s2_ps.at(s, n + 1))
                last_use = n - RING + 1 if n >= RING else n + (A2 - 1 - n) // RING * RING + 1 - A2
                if pv_done.due(s, last_use):
                    act.wait_ge(pv_done.sem, pv_done.at(s, last_use))
                nc.scalar.activation(probs[:, n % RING, 0:w], ps[:, S2B + n % 3, 0:w], ACT.Exp,
                                     scale=HEAD_DIM ** -0.5).then_inc(exped.sem, 1)

            def out_T(s, g):
                act.wait_ge(pv_done.sem, pv_done.at(s, (g + 1) * N2))
                if o_ps.due(s, g - 1):
                    act.wait_ge(o_ps.sem, o_ps.at(s, g - 1))
                copy(oT[:, g % 2, :], ps[:, PVB, :], ot_rdy)

            def attn_T(s, c):
                k = s.plus(-1)
                act.wait_ge(aT_ps.sem, aT_ps.at(k, c + 1))
                if g_ps.due(k, 0):
                    act.wait_ge(g_ps.sem, g_ps.at(k, 0))
                copy(bT[:, c, :], ps[:, misc(s, 8 + c), :], aT_rdy)

            def x2_T(s, c):
                k = s.plus(-1)
                act.wait_ge(x2_ps.sem, x2_ps.at(k, c + 1))
                act.wait_ge(wo_ps.sem, wo_ps.at(k, 2))
                copy(bT[:, c, :], ps[:, misc(s, 15 + c), :], x2_rdy)

            def start(s):
                f = s.plus(1)
                xT(s, 0)
                xT(s, 1)
                act.wait_ge(s_init.sem, N_INIT)
                for t in range(2):
                    high_part(f, t)
                for t in range(2):
                    middle_part(f, t)
                v_half(s, 0)
                v_half(s, 1)
                max_row(f, 0, misc(s, 22))

            def body(s, first, last):
                f = s.plus(1)
                for g in range(G):
                    for k in range(N2):
                        exp_unit(s, g, k)
                        if k == 3 and not (first and g == 0):
                            out_T(s if g else s.plus(-1), (g - 1) % G)
                        if g == 0:
                            if k == 7 and not last:
                                xT(s, 0)
                                xT(s, 1)
                            if k == 8:
                                max_row(s, 1, misc(s, 3))
                        if g == 1:
                            if k == 4 and not first:
                                attn_T(s, 0)
                                attn_T(s, 1)
                            if k in (5, 7) and not last:
                                high_part(f, (k - 5) // 2)
                            if k == 9:
                                max_row(s, 2, misc(s, 11))
                        if g == 2:
                            if k in (0, 2) and not last:
                                middle_part(f, k // 2)
                            if k == 8 and not first:
                                x2_T(s, 0)
                                x2_T(s, 1)
                            if k == 9:
                                max_row(s, 3, misc(s, 17))
                        if g == 3 and not last:
                            if k in (7, 8):
                                v_half(s, k - 7)
                            if k == 9:
                                max_row(f, 0, misc(s, 22))

            def end(s):
                e = s.plus(1)
                out_T(s, G - 1)
                attn_T(e, 0)
                attn_T(e, 1)
                x2_T(e, 0)
                x2_T(e, 1)

            schedule(act, start, body, end)
            with act.Fori(0, NT // RT) as r:
                for u in range(RT):
                    act.wait_ge(xi_ps.sem, r * xi_ps.per + (u + 1))
                    if u >= 2:
                        act.wait_ge(y_ps.sem, r * y_ps.per + (u - 1))
                    copy(xinT[:, u % 2, :, :].rearrange("p c n -> p (c n)"), ps[:, u % 2, 0:D], xi_rdy)

        @block.vector
        def _(dve):
            for p in range(2):
                nc.vector.memset(ks[p][TROWS:TROWS + MROWS, :, :], 1.0).then_inc(s_init.sem, 1)
            for sig in (n_step[1], r_step):
                dve.sem_inc(sig.sem, sig.primed)
            dve.wait_ge(consts.sem, 16 * N_CONST)

            def norm(which, s, src, dst, ready, piece):
                step, st, agg, v = n_step[which], stats[:, which], mv[:, which], nv[:, which]
                done = [0, 1, 2, 3, 4, 8, 9, 10, 13, 16, 19][piece]

                def link(ins):
                    ins.then_inc(step.sem, 1)

                if piece < T:
                    link(nc.vector.bn_stats(st[:, piece, :], src[:, piece, :]))
                elif piece == 4:
                    dve.wait_ge(step.sem, step.at(s, done))
                    dve.sem_inc(waited.sem, 1)
                    for i in range(T):
                        link(nc.vector.bn_aggr(agg[:, i, :], st[:, i, :]))
                elif piece == 5:
                    dve.wait_ge(step.sem, step.at(s, done))
                    link(nc.vector.tensor_scalar(v[:, 0, :], agg[:, :, 1], EPS, None, ALU.add))
                elif piece == 6:
                    dve.wait_ge(step.sem, step.at(s, done))
                    link(nc.vector.tensor_scalar(v[:, 2, :].bitcast(I32), v[:, 0, :].bitcast(I32), -0.5,
                                                 float(0x5F3759DF), ALU.mult, ALU.add))
                elif piece < 10:
                    dve.wait_ge(step.sem, step.at(s, done))
                    link(nc.vector.tensor_tensor(v[:, 1, :], v[:, 2, :], v[:, 2, :], ALU.mult))
                    dve.wait_ge(step.sem, step.at(s, done + 1))
                    link(nc.vector.scalar_tensor_tensor(out=v[:, 3, :], in0=v[:, 1, :], scalar=-0.5,
                                                        in1=v[:, 0, :], op0=ALU.mult, op1=ALU.mult))
                    dve.wait_ge(step.sem, step.at(s, done + 2))
                    link(nc.vector.scalar_tensor_tensor(out=v[:, 2, :], in0=v[:, 3, :], scalar=1.5,
                                                        in1=v[:, 2, :], op0=ALU.add, op1=ALU.mult))
                else:
                    assert done == step.per
                    dve.wait_ge(step.sem, step.at(s, done))
                    for i in range(T):
                        nc.vector.tensor_scalar(dst[:, i, :], src[:, i, :], agg[:, i, 0:1], v[:, 2, i:i + 1],
                                                ALU.subtract, ALU.mult).then_inc(ready.sem, 1)

            def front_norm(f, piece):
                if piece == 0:
                    dve.wait_ge(rows_in.sem, rows_in.at(f, 16 * T))
                if piece == 10:
                    if xt_ps.due(f, 0):
                        dve.wait_ge(xt_ps.sem, xt_ps.at(f, 0))
                norm(0, f, emb[f.parity], xn, xn_rdy, piece)

            def back_norm(k, piece):
                if piece == 0:
                    dve.wait_ge(h2_rdy.sem, h2_rdy.at(k, 2))
                if piece == 10:
                    if xr_free.due(k, 0):
                        dve.wait_ge(xr_free.sem, xr_free.at(k, 0))
                norm(1, k, h2, xn2, xn2_rdy, piece)

            def products(s, t, eos):
                f = s.plus(1)
                for eo in eos:
                    if roped.due(f, 2 * t - 1 + eo):
                        dve.wait_ge(roped.sem, roped.at(f, 2 * t - 1 + eo))
                    for x_ in range(2):
                        dve.wait_ge(qk_ps.sem, qk_ps.at(f, 2 * t + x_ + 1))
                        nc.vector.tensor_tensor(turn[:, 2 * eo + x_, :],
                                                ps[:, misc(s, 4 + 2 * t + x_), :],
                                                trig[:, (eo + x_) % 2, :], ALU.mult).then_inc(turned.sem, 1)

            def maximum(s, g, k):
                i, h0, n = U1[k]
                at = g * N1 + k
                dve.wait_ge(s1_ps.sem, s1_ps.at(s, at + 1))
                nc.vector.tensor_reduce(
                    negm[:, g % 2, i, h0:h0 + n],
                    ps[:, S1B + at % 2, 0:n * (i + 1) * P].rearrange("p (h w) -> p h w", h=n),
                    AX.X, ALU.max, negate=True).then_inc(s1_max.sem, 1)

            def split_max(s, g):
                dve.wait_ge(s1_max.sem, s1_max.at(s, (g + 1) * N1))
                if mt_ps.due(s, g - 1):
                    dve.wait_ge(mt_ps.sem, mt_ps.at(s, g - 1))
                m, r, q = negm[:, g % 2, :, :], mrest[:, g % 2, :, :], mparts[:, g % 2, :, :, :]
                nc.vector.tensor_copy(q[:, :, 0, :], m).then_inc(m_step.sem, 1)
                dve.wait_ge(m_step.sem, m_step.at(s, 3 * g + 1))
                nc.vector.tensor_tensor(r, m, q[:, :, 0, :], ALU.subtract).then_inc(m_step.sem, 1)
                dve.wait_ge(m_step.sem, m_step.at(s, 3 * g + 2))
                nc.vector.tensor_copy(q[:, :, 1, :], r).then_inc(m_step.sem, 1)
                dve.wait_ge(m_step.sem, m_step.at(s, 3 * g + 3))
                nc.vector.tensor_tensor(q[:, :, 2, :], r, q[:, :, 1, :], ALU.subtract).then_inc(m_rdy.sem, 1)

            def divide(s, g, bank):
                dve.wait_ge(o_ps.sem, o_ps.at(s, g + 1))
                o = ps[:, bank, :].rearrange("p (n d) -> p n d", d=2 * HEAD_DIM)
                r = rden[:, g % 2, :]
                nc.vector.reciprocal(r, o[:, :, HEAD_DIM]).then_inc(rd_rdy.sem, 1)
                dve.wait_ge(rd_rdy.sem, rd_rdy.at(s, g + 1))
                if g == 0:
                    if aT_ps.due(s, 0):
                        dve.wait_ge(aT_ps.sem, aT_ps.at(s, 0))
                w = GROUP * HEAD_DIM
                nc.vector.tensor_tensor(
                    attn[:, :, g * w:(g + 1) * w].rearrange("p i (h d) -> p i h d", d=HEAD_DIM),
                    ps[:, bank, :].rearrange("p (i h d) -> p i h d", i=T, d=2 * HEAD_DIM)[:, :, :, 0:HEAD_DIM],
                    r.rearrange("p (i h a) -> p i h a", i=T, a=1).to_broadcast([P, T, GROUP, HEAD_DIM]),
                    ALU.mult).then_inc(at_rdy.sem, 1)

            def residual(s, half):
                k = s.plus(-1)
                dve.wait_ge(wo_ps.sem, wo_ps.at(k, half + 1))
                dve.wait_ge(res_in.sem, res_in.at(k, 16))
                if base.due(k, 0):
                    dve.wait_ge(base.sem, base.at(k, 0))
                nc.vector.tensor_tensor(h2[:, 2 * half:2 * half + 2, :], res[:, 2 * half:2 * half + 2, :],
                                        ps[:, misc(s, 12 + half), :].rearrange("p (i d) -> p i d", i=2),
                                        ALU.add).then_inc(h2_rdy.sem, 1)

            def over(v):
                return v.unsqueeze(2).to_broadcast([P, T, E])

            def choose(s):
                k = s.plus(-1)
                dve.wait_ge(g_ps.sem, g_ps.at(k, 1))
                sc = ps[:, misc(s, 18), 0:T * E].rearrange("p (i e) -> p i e", e=E)
                nc.vector.tensor_reduce(gmax[:, 0, :], sc, AX.X, ALU.max).then_inc(g_step.sem, 1)
                dve.wait_ge(g_step.sem, g_step.at(k, 1))
                nc.vector.tensor_tensor(gate[:, 0, :, :], sc, over(gmax[:, 0, :]), ALU.is_equal)\
                    .then_inc(g_step.sem, 1)
                dve.wait_ge(g_step.sem, g_step.at(k, 2))
                nc.vector.tensor_tensor(gate[:, 1, :, :], gate[:, 0, :, :],
                                        rank[:, :].unsqueeze(1).to_broadcast([P, T, E]), ALU.mult)\
                    .then_inc(g_step.sem, 1)
                dve.wait_ge(g_step.sem, g_step.at(k, 3))
                nc.vector.tensor_reduce(gmax[:, 1, :], gate[:, 1, :, :], AX.X, ALU.max)\
                    .then_inc(g_step.sem, 1)
                dve.wait_ge(g_step.sem, g_step.at(k, 4))
                nc.vector.tensor_tensor(onehot[:, :, :], gate[:, 1, :, :], over(gmax[:, 1, :]),
                                        ALU.is_equal).then_inc(g_step.sem, 1)

            def positions(s):
                k = s.plus(-1)
                nc.vector.tensor_copy(xr[:, :, 2 * D:W].bitcast(I32),
                                      tok[:, :].unsqueeze(2).to_broadcast([P, T, W - 2 * D]))\
                    .then_inc(r_step.sem, 1)
                dve.wait_ge(r_ps.sem, r_ps.at(k, 1))
                bank = misc(s, 18)
                rk = ps[:, bank, T * E:2 * T * E].rearrange("p (i e) -> p i e", e=E)
                nc.vector.tensor_tensor(slot[:, 0, :, :], rk, cnt[:, :].unsqueeze(1).to_broadcast([P, T, E]),
                                        ALU.add).then_inc(r_step.sem, 1)
                dve.wait_ge(r_step.sem, r_step.at(k, 2))
                nc.vector.tensor_tensor(cnt[:, :], cnt[:, :], ps[:, bank, 2 * T * E:2 * T * E + E], ALU.add)\
                    .then_inc(r_step.sem, 1)
                nc.vector.tensor_scalar(tok[:, :], tok[:, :], float(S), None, ALU.add).then_inc(r_step.sem, 1)
                nc.vector.tensor_tensor(slot[:, 1, :, :], slot[:, 0, :, :], onehot[:, :, :], ALU.mult)\
                    .then_inc(r_step.sem, 1)
                dve.wait_ge(r_step.sem, r_step.at(k, 5))
                nc.vector.tensor_reduce(pos[:, 0, :], slot[:, 1, :, :], AX.X, ALU.add).then_inc(r_step.sem, 1)
                dve.wait_ge(r_step.sem, r_step.at(k, 6))
                nc.vector.tensor_copy(pos[:, 1, :].bitcast(I32), pos[:, 0, :]).then_inc(p_rdy.sem, 1)

            def start(s):
                f = s.plus(1)
                for piece in range(11):
                    front_norm(f, piece)
                for t in range(2):
                    products(s, t, (0, 1))
                for k in range(N1):
                    maximum(f, 0, k)
                split_max(f, 0)

            def body(s, first, last):
                f, b = s.plus(1), s.plus(-1)
                for g in range(G):
                    ahead = (s, g + 1) if g + 1 < G else (f, 0)
                    if g == 2 and not first:
                        residual(s, 0)
                        residual(s, 1)
                    if g == 3 and not first:
                        choose(s)
                    for k in range(N1):
                        if not (last and g == 3):
                            maximum(*ahead, k)
                        if g == 0 and not last:
                            front_norm(f, k)
                        if g == 1 and k in (2, 3) and not last:
                            products(s, 1, (k - 2,))
                        if g == 2 and not first:
                            back_norm(b, k)
                    if not (last and g == 3):
                        split_max(*ahead)
                    if g == 0:
                        if not first:
                            divide(b, G - 1, misc(s, 0))
                        if not last:
                            products(s, 0, (0, 1))
                    else:
                        divide(s, g - 1, misc(s, (None, 10, 14, 19)[g]))
                    if g == 3 and not first:
                        positions(s)

            def end(s):
                e = s.plus(1)
                divide(s, G - 1, misc(e, 0))
                residual(e, 0)
                residual(e, 1)
                for piece in range(11):
                    back_norm(s, piece)
                choose(e)
                positions(e)

            schedule(dve, start, body, end)

            k = [0]

            def step(ins):
                ins.then_inc(t_step.sem, 1)
                k[0] += 1
                dve.wait_ge(t_step.sem, k[0])

            def cut(at, n):
                return tab[:, at:at + n]

            dve.wait_ge(pv_done.sem, B * pv_done.per)
            starts = cut(0, E)
            fills = cut(E, 32)
            below = cut(E + 32, E * E).rearrange("p (e f) -> p e f", f=E)
            number = cut(E + 32 + E * E, NT)
            first = cut(E + 32 + E * E + NT, NT)
            counts, per, ends = tn[:, 0, 0:E], tn[:, 1, 0:E], tn[:, 2, 0:E]
            expert, begun, row, low_row = tn[:, 3, :], tn[:, 4, :], tn[:, 5, :], tn[:, 6, :]
            step(nc.vector.memset(pad, 1.0))
            step(nc.vector.tensor_copy(cnt_i[:, :], cnt[0:1, :]))
            step(nc.vector.tensor_tensor(counts, cnt[0:1, :], starts, ALU.subtract))
            f = tw[:, 0, 0:E * 32].rearrange("p (e k) -> p e k", k=32)
            step(nc.vector.tensor_tensor(f, counts.unsqueeze(2).to_broadcast([1, E, 32]),
                                         fills.unsqueeze(1).to_broadcast([1, E, 32]), ALU.is_gt))
            step(nc.vector.tensor_reduce(per, f, AX.X, ALU.add))
            t = tw[:, 1, 0:E * E].rearrange("p (e f) -> p e f", f=E)
            step(nc.vector.tensor_tensor(t, below, per.unsqueeze(1).to_broadcast([1, E, E]), ALU.mult))
            step(nc.vector.tensor_reduce(ends, t, AX.X, ALU.add))
            o = tw[:, 2, :].rearrange("p (j e) -> p j e", e=E)
            step(nc.vector.tensor_tensor(o, ends.unsqueeze(1).to_broadcast([1, NT, E]),
                                         number.unsqueeze(2).to_broadcast([1, NT, E]), ALU.is_le))
            step(nc.vector.tensor_reduce(expert, o, AX.X, ALU.add))
            w = tw[:, 3, :].rearrange("p (j e) -> p j e", e=E)
            step(nc.vector.tensor_tensor(w, o, per.unsqueeze(1).to_broadcast([1, NT, E]), ALU.mult))
            step(nc.vector.tensor_reduce(begun, w, AX.X, ALU.add))
            step(nc.vector.scalar_tensor_tensor(out=low_row, in0=begun, scalar=float(-P), in1=first,
                                                op0=ALU.mult, op1=ALU.add))
            step(nc.vector.scalar_tensor_tensor(out=row, in0=expert, scalar=float(CAP), in1=low_row,
                                                op0=ALU.mult, op1=ALU.add))
            step(nc.vector.tensor_scalar(tiles[:, 0, :], row, float(E * CAP), None, ALU.min))
            step(nc.vector.tensor_scalar(tiles[:, 1, :], expert, float(E - 1), None, ALU.min))
            assert k[0] == N_TSTEP
            with dve.Fori(0, NT // RT) as r:
                for u in range(RT):
                    dve.wait_ge(y_ps.sem, r * y_ps.per + (u + 1))
                    nc.vector.tensor_tensor(y[:, u, :], ps[:, 2 + u % 2, 0:D], xin[:, u, D:2 * D],
                                            ALU.add).then_inc(y_rdy.sem, 1)

        @block.tensor
        def _(pe):
            for sig in (aT_ps, g_ps):
                pe.sem_inc(sig.sem, sig.primed)
            pe.wait_ge(consts.sem, 16 * N_CONST)
            pe.wait_ge(s_init.sem, N_INIT)

            def turn_rows(src, bank, c, done):
                for i in range(T):
                    mm = pe.transpose(ps[:, bank, i * P:(i + 1) * P], src[:, i, c * P:(c + 1) * P], idf[:, :])
                mm.then_inc(done.sem, 1)

            def turn_xn(s, c):
                f = s.plus(1)
                pe.wait_ge(xn_rdy.sem, xn_rdy.at(f, T))
                if c == 0 and mt_rdy.due(s, 1):
                    pe.wait_ge(mt_rdy.sem, mt_rdy.at(s, 1))
                if c == 1 and at_rdy.due(s, 0):
                    pe.wait_ge(at_rdy.sem, at_rdy.at(s, 0))
                if c == 1 and v_rdy.due(s, 2):
                    pe.wait_ge(v_rdy.sem, v_rdy.at(s, 2))
                turn_rows(xn, misc(s, 1 + c), c, xt_ps)

            def project_qk(s, n):
                f = s.plus(1)
                if n == 0:
                    pe.wait_ge(xt_rdy.sem, xt_rdy.at(f, C))
                elif n == 1 and mt_rdy.due(s, 2):
                    pe.wait_ge(mt_rdy.sem, mt_rdy.at(s, 2))
                elif n >= 2:
                    pe.wait_ge(turned.sem, turned.at(f, n + 1))
                for c in range(C):
                    mm = pe.matmul(ps[:, misc(s, 4 + n), :], wqk[:, c, n, :], xnT[:, c, :],
                                   start=(c == 0), stop=(c == C - 1))
                mm.then_inc(qk_ps.sem, 1)

            def tokens_by(src, w, bank, half, done):
                for i in range(2):
                    for c in range(C):
                        at = (2 * half + i) * P
                        mm = pe.matmul(ps[:, bank, i * D:(i + 1) * D], src[:, c, at:at + P], w[:, c, :],
                                       start=(c == 0), stop=(c == C - 1))
                mm.then_inc(done.sem, 1)

            def project_v(s, half, first):
                if half:
                    pe.wait_ge(at_rdy.sem, at_rdy.at(s, 3))
                elif first:
                    pe.wait_ge(at_rdy.sem, at_rdy.at(s, 2))
                else:
                    if r_step.due(s, 0):
                        pe.wait_ge(r_step.sem, r_step.at(s, 0))
                tokens_by(xnT, wv, misc(s, 20 + half), half, v_ps)

            def turn_max(s, g, bank):
                pe.wait_ge(m_rdy.sem, m_rdy.at(s, g + 1))
                view = ps[0:MROWS * GROUP, bank, 0:S // 2].bitcast(BF16)
                for i in range(T):
                    mm = pe.transpose(view[:, i * P:(i + 1) * P],
                                      mparts[:, g % 2, i, :, :].rearrange("p a h -> p (a h)"), idb[:, :])
                mm.then_inc(mt_ps.sem, 1)

            def turn_out(s, g, bank):
                pe.wait_ge(ot_rdy.sem, ot_rdy.at(s, g + 1))
                for i in range(T):
                    mm = pe.transpose(ps[:, bank, i * P:(i + 1) * P], oT[:, g % 2, i * P:(i + 1) * P], idf[:, :])
                mm.then_inc(o_ps.sem, 1)

            def pass1_unit(s, g, k):
                i, h0, n = U1[k]
                at = g * N1 + k
                w = (i + 1) * P
                bank = S1B + at % 2
                if at == 0:
                    pe.wait_ge(stacked.sem, stacked.at(s, stacked.per))
                if s1_max.due(s, at - 1):
                    pe.wait_ge(s1_max.sem, s1_max.at(s, at - 1))
                q, kk = qs[s.parity], ks[s.parity]
                for x_ in range(n):
                    hd = g * GROUP + h0 + x_
                    pe.matmul(ps[:, bank, x_ * w:(x_ + 1) * w], q[0:TROWS, hd, i * P:(i + 1) * P],
                              kk[0:TROWS, hd, 0:w], start=True, stop=False)
                    mm = pe.matmul(ps[:, bank, (x_ + 1) * w - P:(x_ + 1) * w], idb[:, :],
                                   causal[:, :], start=False, stop=True)
                mm.then_inc(s1_ps.sem, 1)

            def pass2_unit(s, g, k):
                j, h0, n = U2[k]
                at = g * N2 + k
                w = (T - j) * P
                if k == 0:
                    pe.wait_ge(m_in[g % 2].sem, m_in[g % 2].at(s, 16 * (g // 2 + 1)))
                if exped.due(s, at - 2 if at >= 3 else (-1, 0, -2)[at]):
                    pe.wait_ge(exped.sem, exped.at(s, at - 2 if at >= 3 else (-1, 0, -2)[at]))
                for x_ in range(n):
                    hd = g * GROUP + h0 + x_
                    mm = pe.matmul(ps[:, S2B + at % 3, x_ * w:(x_ + 1) * w],
                                   ks[s.parity][:, hd, j * P:(j + 1) * P], qs[s.parity][:, hd, j * P:S],
                                   start=True, stop=True)
                mm.then_inc(s2_ps.sem, 1)

            def pv(s, g, j):
                if j == 0:
                    if ot_rdy.due(s, g):
                        pe.wait_ge(ot_rdy.sem, ot_rdy.at(s, g))
                    pe.wait_ge(v_rdy.sem, v_rdy.at(s, 2))
                units = [k for k, u in enumerate(U2) if u[0] == j]
                pe.wait_ge(masked.sem, masked.at(s, g * N2 + units[-1] + 1))
                for k in units:
                    _, h0, nh = U2[k]
                    pr = p_unit(g * N2 + k, U2[k])
                    for x_ in range(nh):
                        hh = h0 + x_
                        mm = pe.matmul(ps[32 * hh:32 * hh + 32, PVB, j * P:S],
                                       vaug[s.parity][:, j, g * GROUP + hh, :], pr[:, x_, :],
                                       start=(j == 0), stop=(j == T - 1))
                    mm.then_inc(pv_done.sem, 1)

            def gates(s):
                k = s.plus(-1)
                pe.wait_ge(x2_rdy.sem, x2_rdy.at(k, C))
                for i in range(T):
                    for c in range(C):
                        mm = pe.matmul(ps[:, misc(s, 18), i * E:(i + 1) * E], bT[:, c, i * P:(i + 1) * P],
                                       wg[:, c, :], start=(c == 0), stop=(c == C - 1))
                mm.then_inc(g_ps.sem, 1)

            def ranks(s):
                pe.wait_ge(g_step.sem, g_step.at(s.plus(-1), g_step.per))
                for i in range(T + 1):
                    for j in range(min(i + 1, T)):
                        mm = pe.matmul(ps[:, misc(s, 18), (T + i) * E:(T + i + 1) * E],
                                       before[:, 0 if i == j else 1, :], onehot[:, j, :],
                                       start=(j == 0), stop=(j == min(i, T - 1)))
                mm.then_inc(r_ps.sem, 1)

            def start(s):
                f = s.plus(1)
                turn_xn(s, 0)
                turn_xn(s, 1)
                for n in range(4):
                    project_qk(s, n)
                pe.wait_ge(turned.sem, turned.at(f, 8))
                tokens_by(xnT, wv, misc(s, 20), 0, v_ps)
                tokens_by(xnT, wv, misc(s, 21), 1, v_ps)
                for k in range(N1):
                    pass1_unit(f, 0, k)
                pe.wait_ge(v_rdy.sem, v_rdy.at(f, 2))
                turn_max(f, 0, misc(s, 22))

            def body(s, first, last):
                f, b = s.plus(1), s.plus(-1)
                for g in range(G):
                    ahead = (s, g + 1) if g + 1 < G else (f, 0)
                    for k in range(N2):
                        pass2_unit(s, g, k)
                        if k in (1, 2) and not (first and g == 0):
                            pv(s if g else b, (g - 1) % G, k + 1)
                        if k < 6 and not (last and g == 3):
                            for u in range(2 * k, min(2 * k + 2, N1)):
                                pass1_unit(*ahead, u)
                        if k == 5:
                            pv(s, g, 0)
                        if k == 9:
                            pv(s, g, 1)
                        if g == 0:
                            if k == 5 and not first:
                                pe.wait_ge(v_rdy.sem, v_rdy.at(s, 2))
                                turn_out(b, G - 1, misc(s, 0))
                            if k == 6 and not last:
                                turn_xn(s, 0)
                                turn_xn(s, 1)
                            if k == 7:
                                if not last:
                                    pe.wait_ge(xt_rdy.sem, xt_rdy.at(f, 1))
                                pe.wait_ge(mt_rdy.sem, mt_rdy.at(s, 1))
                                turn_max(s, 1, misc(s, 3))
                            if k in (8, 9) and not last:
                                project_qk(s, k - 8)
                        if g == 1:
                            if k in (0, 1) and not last:
                                project_qk(s, k + 2)
                            if k == 3 and not first:
                                if not last:
                                    pe.wait_ge(turned.sem, turned.at(f, 8))
                                pe.wait_ge(mt_rdy.sem, mt_rdy.at(s, 2))
                                pe.wait_ge(at_rdy.sem, at_rdy.at(b, G))
                                for c in range(C):
                                    turn_rows(attn, misc(s, 8 + c), c, aT_ps)
                            if k == 5:
                                if first:
                                    pe.wait_ge(turned.sem, turned.at(f, 8))
                                else:
                                    pe.wait_ge(aT_rdy.sem, aT_rdy.at(b, 1))
                                turn_out(s, 0, misc(s, 10))
                            if k == 8:
                                if first:
                                    pe.wait_ge(turned.sem, turned.at(f, 8))
                                else:
                                    pe.wait_ge(aT_rdy.sem, aT_rdy.at(b, 2))
                                turn_max(s, 2, misc(s, 11))
                            if k in (9, 10) and not first:
                                if k == 9:
                                    pe.wait_ge(aT_rdy.sem, aT_rdy.at(b, C))
                                    pe.wait_ge(at_rdy.sem, at_rdy.at(s, 1))
                                else:
                                    pe.wait_ge(mt_rdy.sem, mt_rdy.at(s, 3))
                                tokens_by(bT, wo, misc(s, 3 + k), k - 9, wo_ps)
                        if g == 2:
                            if k == 5:
                                if first:
                                    pe.wait_ge(at_rdy.sem, at_rdy.at(s, 1))
                                else:
                                    pe.wait_ge(h2_rdy.sem, h2_rdy.at(b, 1))
                                turn_out(s, 1, misc(s, 14))
                            if k == 7 and not first:
                                pe.wait_ge(xn2_rdy.sem, xn2_rdy.at(b, T))
                                pe.wait_ge(h2_rdy.sem, h2_rdy.at(b, 2))
                                turn_rows(xn2, misc(s, 15), 0, x2_ps)
                                pe.wait_ge(at_rdy.sem, at_rdy.at(s, 2))
                                turn_rows(xn2, misc(s, 16), 1, x2_ps)
                            if k == 8:
                                if first:
                                    pe.wait_ge(mt_rdy.sem, mt_rdy.at(s, 3))
                                else:
                                    pe.wait_ge(x2_rdy.sem, x2_rdy.at(b, 1))
                                turn_max(s, 3, misc(s, 17))
                            if k == 10 and not first:
                                gates(s)
                        if g == 3:
                            if k == 1 and not first:
                                ranks(s)
                            if k == 5:
                                pe.wait_ge(mt_rdy.sem, mt_rdy.at(s, 4))
                                turn_out(s, 2, misc(s, 19))
                            if k in (6, 7) and not last:
                                project_v(s, k - 6, first)
                            if k == 8 and not last:
                                pe.wait_ge(v_rdy.sem, v_rdy.at(f, 1))
                                turn_max(f, 0, misc(s, 22))

            def end(s):
                e = s.plus(1)
                pv(s, G - 1, 2)
                pv(s, G - 1, 3)
                pe.wait_ge(at_rdy.sem, at_rdy.at(s, 3))
                if r_step.due(s, 0):
                    pe.wait_ge(r_step.sem, r_step.at(s, 0))
                turn_out(s, G - 1, misc(e, 0))
                pe.wait_ge(at_rdy.sem, at_rdy.at(s, G))
                for c in range(C):
                    turn_rows(attn, misc(e, 8 + c), c, aT_ps)
                pe.wait_ge(aT_rdy.sem, aT_rdy.at(s, C))
                for half in range(2):
                    tokens_by(bT, wo, misc(e, 12 + half), half, wo_ps)
                pe.wait_ge(xn2_rdy.sem, xn2_rdy.at(s, T))
                for c in range(C):
                    turn_rows(xn2, misc(e, 15 + c), c, x2_ps)
                gates(e)
                ranks(e)

            schedule(pe, start, body, end)

            pe.wait_ge(t_step.sem, N_TSTEP)
            with pe.Fori(0, NT // RT) as r:
                def turn_tile(u):
                    pe.wait_ge(tile_in[u].sem, r * 16 + 16)
                    if u >= 2:
                        pe.wait_ge(xi_rdy.sem, r * xi_rdy.per + (u - 1))
                    for c in range(C):
                        mm = pe.transpose(ps[:, u % 2, c * P:(c + 1) * P], xin[:, u, c * P:(c + 1) * P],
                                          idf[:, :])
                    mm.then_inc(xi_ps.sem, 1)

                turn_tile(0)
                for u in range(RT):
                    if u + 1 < RT:
                        turn_tile(u + 1)
                    pe.wait_ge(xi_rdy.sem, r * xi_rdy.per + (u + 1))
                    if u >= 2:
                        pe.wait_ge(y_rdy.sem, r * y_rdy.per + (u - 1))
                    e = pe.value_load(tiles[0:1, 1, bass.ds(r * RT + u, 1)], min_val=0, max_val=E - 1)
                    for c in range(C):
                        mm = pe.matmul(ps[:, 2 + u % 2, 0:D], xinT[:, u % 2, c, :],
                                       we[:, c, bass.ds(e, 1), :].rearrange("p a d -> p (a d)"),
                                       start=(c == 0), stop=(c == C - 1))
                    mm.then_inc(y_ps.sem, 1)


def kernel(x, L0_tok_weight, L0_attn_W_qkv, L0_attn_W_o, L0_ffn_gate_w, L0_ffn_expert_w):
    import ml_dtypes
    import concourse.bacc as bacc
    from concourse.bass_utils import run_bass_kernel_spmd

    D = L0_tok_weight.shape[1]
    B, S = x.shape
    E = L0_ffn_gate_w.shape[0]
    C = D // P

    def chunks(w_t):
        return np.ascontiguousarray(w_t.reshape(C, P, -1).transpose(1, 0, 2))

    wqkv = np.asarray(L0_attn_W_qkv)
    w_qk = np.stack([wqkv[t * D:(t + 1) * D].reshape(HEADS, PAIRS, 2, D)[:, :, eo].transpose(1, 0, 2).reshape(P, D)
                     for t in range(2) for eo in range(2)])
    w_qk = np.ascontiguousarray(w_qk.transpose(2, 0, 1).reshape(C, P, 4, P).transpose(1, 0, 2, 3))
    w_exp = np.asarray(L0_ffn_expert_w).transpose(2, 0, 1).reshape(C, P, E, D).transpose(1, 0, 2, 3)

    inv = np.float32(ROPE_THETA) ** (np.arange(0, HEAD_DIM, 2, dtype=np.float32) / np.float32(HEAD_DIM))
    ang = np.arange(S, dtype=np.float32)[None, :] / inv[:, None].astype(np.float32)
    cos, sin = (np.repeat(f(ang).astype(np.float32), HEADS, axis=0) for f in (np.cos, np.sin))
    rope = np.stack([cos, sin], axis=1)
    ident = np.eye(P, dtype=np.float32)
    upper = np.triu(np.full((P, P), NEG, np.float32), 1).astype(ml_dtypes.bfloat16)
    cap = B * S + P
    nt = B * S // P + E
    before = np.stack([np.triu(np.ones((P, P)), 1), np.ones((P, P))], axis=1).astype(ml_dtypes.bfloat16)
    cnt = np.tile(np.arange(E, dtype=np.float32) * cap, (P, 1))
    tok = np.ascontiguousarray(np.arange(S, dtype=np.float32).reshape(S // P, P).T)
    tab = np.concatenate([np.arange(E) * cap, np.arange(32) * P, np.tril(np.ones((E, E))).ravel(),
                          np.arange(nt), np.arange(nt) * P])[None].astype(np.float32)
    rank = np.tile(np.arange(E, 0, -1, dtype=np.float32), (P, 1))

    arrays = {
        "x": np.ascontiguousarray(np.asarray(x).reshape(B, S // P, P).transpose(2, 0, 1)),
        "weight": np.ascontiguousarray(L0_tok_weight),
        "w_qk": w_qk, "w_v": chunks(wqkv[2 * D:].T), "w_o": chunks(np.asarray(L0_attn_W_o).T),
        "w_gate": chunks(np.asarray(L0_ffn_gate_w).T), "w_exp": np.ascontiguousarray(w_exp),
        "rope": rope, "ident": ident, "identb": ident.astype(ml_dtypes.bfloat16), "mask": upper, "rank": rank,
        "before": before, "cnt": cnt, "tok": tok, "tab": tab,
    }
    nc = bacc.Bacc("TRN2", target_bir_lowering=False, num_devices=1)
    t = {n: nc.dram_tensor(f"in_{n}", a.shape, mybir.dt.from_np(a.dtype), kind="ExternalInput").ap()
         for n, a in arrays.items()}
    out = nc.dram_tensor("out", (B, S, D), F32, kind="ExternalOutput").ap()
    tower(nc, t["x"], t["weight"], t["w_qk"], t["w_v"], t["w_o"], t["w_gate"], t["w_exp"], t["rope"],
          t["ident"], t["identb"], (t["mask"], t["rank"]), (t["before"], t["cnt"], t["tok"], t["tab"]), out)
    r = run_bass_kernel_spmd(nc, [{f"in_{n}": a for n, a in arrays.items()}], core_ids=[0])
    return r.results[0]["out"]
```

```python
from contextlib import ExitStack

import numpy as np

import concourse.bass as bass
from concourse import mybir

F32 = mybir.dt.float32
BF16 = mybir.dt.bfloat16
I32 = mybir.dt.int32
U32 = mybir.dt.uint32
ALU = mybir.AluOpType
ACT = mybir.ActivationFunctionType
AX = mybir.AxisListType

P = 128
HEADS = 16
HEAD_DIM = 16
PAIRS = HEAD_DIM // 2
EPS = 1e-5
ROPE_THETA = 10000.0
NEG = -1e30
GROUP = 4
TERMS = [(0, 0), (0, 1), (0, 2), (1, 0), (1, 1), (2, 0)]
TROWS = len(TERMS) * HEAD_DIM
MROWS = 3


class Seq:

    def __init__(self, c, q=None):
        self.c, self.q = c, q
        self.index = c if q is None else 2 * q + c
        self.parity = c % 2

    def plus(self, n):
        return Seq(self.c + n, self.q)


class Signal:

    def __init__(self, sem, per, primed=0):
        self.sem, self.per, self.primed = sem, per, primed

    def due(self, s, n):
        return s.q is not None or s.c * self.per + n > 0

    def at(self, s, n):
        value = s.c * self.per + n + self.primed
        assert value > 0, "nothing to wait for, or prime it"
        return value if s.q is None else s.index * self.per + (n + self.primed)


def tower(nc, x, weight, w_qk, w_v, w_o, w_gate, w_exp, rope, ident, identb, mask, tables, out):
    B, S, _ = out.shape
    DEPTH, D = weight.shape
    C = D // P
    T = S // P
    E = w_gate.shape[2]
    G = HEADS // GROUP
    CAP = P + B * S
    W = 2 * D + 4
    NT = B * S // P + E
    NA = ((B - 1) * S // P - (E - 1)) // 4 * 4
    RT = 8
    RA = -(-NA // RT)
    assert NT % RT == 0 and RA < NT // RT and B % 2 == 0 and S == 512

    U1, U2 = [], []
    for i in range(T):
        n = min(GROUP, 512 // ((i + 1) * P))
        U1 += [(i, h, n) for h in range(0, GROUP, n)]
    for j in range(T):
        n = min(GROUP, 512 // ((T - j) * P))
        U2 += [(j, h, n) for h in range(0, GROUP, n)]
    N1, N2 = len(U1), len(U2)
    A1, A2 = N1 * G, N2 * G
    RING = 8
    assert N1 == N2 == 11
    LEAD = N1 + 7
    S1B, S2B, PVB, MB = 0, 3, 5, 6
    YB = (2, 3)

    with ExitStack() as ctx:
        def sb(name, shape, dt=F32):
            return ctx.enter_context(nc.sbuf_tensor(name, shape, dt))

        def signal(name, per, primed=0):
            return Signal(ctx.enter_context(nc.semaphore(name)), per, primed)

        wqk = sb("wqk", [P, C, 4, P])
        wv = sb("wv", [P, C, D])
        wo = sb("wo", [P, C, D])
        wg = sb("wg", [P, C, E])
        we = sb("we", [P, C, E, D])
        trig = sb("trig", [P, 2, S])
        idf = sb("idf", [P, P])
        idb = sb("idb", [P, P], BF16)
        causal = sb("causal", [P, P], BF16)
        rank = sb("rank", [P, E])
        before = sb("before", [P, 2, P], BF16)
        cnt = sb("cnt", [P, E])
        pad = sb("pad", [P, W // 4])
        tok = sb("tok", [P, T])
        tab = sb("tab", [1, E + 64 + E * E + 2 * NT])
        ids_all = sb("ids_all", [P, B + 1, T], I32)

        ids = sb("ids", [P, T], I32)
        emb = [sb(f"emb{p}", [P, T, D]) for p in range(2)]
        stats = sb("stats", [P, 2, T, 6])
        mv = sb("mv", [P, 2, T, 2])
        nv = sb("nv", [P, 2, 4, T])
        xn = sb("xn", [P, T, D])
        xnT = sb("xnT", [P, C, S])
        turn = sb("turn", [P, 4, S])
        qk = sb("qk", [P, 2, 2, S])
        parts = sb("parts", [P, 3, 2, 2, S], BF16)
        qs = [sb(f"qs{p}", [TROWS + MROWS, HEADS, S], BF16) for p in range(2)]
        ks = [sb(f"ks{p}", [TROWS + MROWS, HEADS, S], BF16) for p in range(2)]
        VN = T * HEADS * 2 * HEAD_DIM
        vbuf = sb("vbuf", [P, max(2 * VN, RT * W)])
        vaug = [vbuf[:, p * VN:(p + 1) * VN].rearrange("p (i h d) -> p i h d", i=T, h=HEADS)
                for p in range(2)]

        negm = sb("negm", [P, 2, T, GROUP])
        mrest = sb("mrest", [P, 2, T, GROUP])
        mparts = sb("mparts", [P, 2, T, MROWS, GROUP], BF16)
        mrow = sb("mrow", [MROWS * GROUP, 2, S], BF16)
        probs = sb("probs", [P, RING, 512])
        oT = sb("oT", [P, 2, S])
        rden = sb("rden", [P, 2, T * GROUP])
        attn = sb("attn", [P, T, D])

        res = [sb(f"res{p}", [P, T, D]) for p in range(2)]
        bT = sb("bT", [P, C, S])
        h2 = sb("h2", [P, T, D])
        gate = sb("gate", [P, 2, T, E])
        gmax = sb("gmax", [P, 2, T])
        xr = sb("xr", [P, T, W])
        xn2 = xr[:, :, 0:D]
        onehot = sb("onehot", [P, T, E], BF16)
        slot = sb("slot", [P, 2, T, E])
        pos = sb("pos", [P, 2, T])

        done = sb("done", [1, E])
        shift = sb("shift", [1, E + 1])
        tiles = sb("tiles", [1, 2, NT], I32)
        tw = turn[0:1, :, 0:NT * E]
        tn = qk[0:1, 0, :, :].rearrange("p a s -> p (a s)")[:, 0:8 * NT].rearrange("p (a n) -> p a n", n=NT)
        y = probs[:, 4:8, :].rearrange("p a (b d) -> p (a b) d", d=D)
        xin = vbuf[:, 0:RT * W].rearrange("p (u w) -> p u w", w=W)
        xinT = xnT.rearrange("p c s -> p (c s)")[:, 0:2 * D].rearrange("p (u c n) -> p u c n", u=2, c=C)

        ps = ctx.enter_context(nc.psum_tensor("ps", [P, 8, 512], F32))

        NORM_STEPS = 2 * T + 2 + 3 * 3
        ids_in = signal("ids_in", 0)
        consts = signal("front_consts", 0)
        consts2 = signal("later_consts", 0)
        experts_in = signal("experts_in", 0)
        s_init = signal("init", 0)
        no_ids = signal("dummy_ids", 0)
        ids_cp = signal("ids_copied", 1)
        emb_zero = signal("emb_zero", 1)
        rows_in = signal("rows_in", 16 * T)
        res_in = signal("residual_in", 16)
        n_step = [signal("front_norm_step", NORM_STEPS), signal("back_norm_step", NORM_STEPS, 1)]
        xn_rdy = signal("xn_ready", T)
        xt_ps = signal("xT_in_psum", C)
        xt_rdy = signal("xT_ready", C)
        qk_ps = signal("qk_in_psum", 4)
        v_ps = signal("v_in_psum", 2)
        v_rdy = signal("v_ready", 2)
        turned = signal("rope_products", 8)
        roped = signal("rope_sums", 4)
        high = signal("high_parts", 2)
        less = signal("rests", 2)
        middle = signal("middle_parts", 2)
        low = signal("low_parts", 2)
        stacked = signal("stacked", 16 * 4 * len(TERMS))
        s1_ps = signal("scores_in_psum", A1)
        s1_max = signal("maxima", A1)
        m_step = signal("maxima_split_step", 3 * G)
        m_rdy = signal("maxima_split", G)
        mt_ps = signal("maxT_in_psum", G)
        mt_rdy = signal("maxT_ready", G)
        m_in = [signal(f"max_rows_in{p}", 16 * G // 2) for p in range(2)]
        s2_ps = signal("scoresT_in_psum", A2)
        exped = signal("exp_done", A2)
        masked = signal("probs_masked", A2)
        pv_done = signal("pv_done", A2)
        ot_rdy = signal("oT_ready", G)
        o_ps = signal("o_in_psum", G)
        rd_rdy = signal("denominators", G)
        at_rdy = signal("attn_ready", G)
        aT_ps = signal("attnT_in_psum", C, 1)
        aT_rdy = signal("attnT_ready", C)
        wo_ps = signal("proj_in_psum", 2)
        h2_rdy = signal("h2_ready", 2, 1)
        xn2_rdy = signal("xn2_ready", T)
        x2_ps = signal("x2T_in_psum", C)
        x2_rdy = signal("x2T_ready", C)
        g_ps = signal("gates_in_psum", 1, 1)
        g_step = signal("gate_step", 5)
        base = signal("base_ready", T, 1)
        r_ps = signal("ranks_in_psum", 1)
        r_step = signal("route_step", 6, 1)
        p_rdy = signal("positions_ready", 1)
        routed = signal("rows_routed", 16 * T)
        xr_free = signal("routed_rows_free", 1, 1)
        pad_set = signal("pad_set", 0)
        padded = signal("pads_written", 0)
        ta_step = signal("first_tiles_step", 0)
        tb_step = signal("later_tiles_step", 0)
        tile_in = [signal(f"tile{u}_in", 16) for u in range(RT)]
        xi_ps = signal("tileT_in_psum", RT)
        xi_rdy = signal("tileT_ready", RT)
        y_ps = signal("y_in_psum", RT, 2)
        y_rdy = signal("y_ready", RT, 2)
        y_out = [signal(f"y{u}_scattered", 16) for u in range(RT)]
        waited = signal("waited", 0)

        block = ctx.enter_context(nc.Block())
        N_CONST, N_CONST2 = 4, 11
        N_TA, N_TB = 17, 16
        N_INIT = 2
        routed_rows = nc.dram_tensor("routed_rows", (E * CAP + P, W), F32, kind="Internal").ap()
        out_rows = out.rearrange("b s d -> (b s) d")


        def schedule(engine, before_first, body, after_last):
            before_first(Seq(-1))
            body(Seq(0), True, False)
            with engine.Fori(0, B // 2 - 1) as q:
                body(Seq(1, q), False, False)
                body(Seq(2, q), False, False)
            body(Seq(B - 1), False, True)
            after_last(Seq(B - 1))

        def p_unit(k, u):
            j, _, n = u
            w = (T - j) * P
            return probs[:, k % RING, 0:n * w].rearrange("p (h w) -> p h w", w=w)

        def value(sig, rd, n):
            c, r = rd
            base_value = c * sig.per + n + sig.primed
            return base_value if r is None else r * sig.per + base_value

        def stack(engine, f, part, t):
            part_rdy = (high, middle, low)[part]
            engine.wait_ge(part_rdy.sem, part_rdy.at(f, t + 1))
            dst = (qs, ks)[t][f.parity]
            for n, term in enumerate(TERMS):
                if term[t] == part:
                    for eo in range(2):
                        r = n * HEAD_DIM + eo * PAIRS
                        engine.dma_start(dst[r:r + PAIRS, :, :], parts[:, part, t, eo, :])\
                            .then_inc(stacked.sem, 16)

        def tile_no(rd, u):
            return rd[0] * RT + u if rd[1] is None else rd[1] * RT + (rd[0] * RT + u)

        def later_tiles(engine, tile):
            for n in range(NA, RA * RT):
                tile((n // RT, None), n % RT)
            with engine.Fori(0, NT // RT - RA) as r:
                for u in range(RT):
                    tile((RA, r), u)

        def misc(m):
            return MB + m % 2

        @block.sync
        def _(sp):
            sp.dma_start(ids_all[:, 0:B, :], x).then_inc(ids_in.sem, 16)
            for dst, src in ((idf, ident), (wqk, w_qk), (trig, rope), (wv, w_v)):
                sp.dma_start(dst[:], src).then_inc(consts.sem, 16)
            for dst, src in ((idb, identb), (causal, mask[0]), (rank, mask[1]),
                             (before, tables[0]), (cnt, tables[1]), (tok, tables[2]), (tab, tables[3]), (wg, w_gate)):
                sp.dma_start(dst[:], src).then_inc(consts2.sem, 16)
            for p in range(2):
                sp.dma_start(ks[p][TROWS:TROWS + MROWS, :, :], tables[4]).then_inc(consts2.sem, 16)

            def max_rows(s, g):
                sp.wait_ge(mt_rdy.sem, mt_rdy.at(s, g + 1))
                sp.dma_start(qs[s.parity][TROWS:TROWS + MROWS, g * GROUP:(g + 1) * GROUP, :],
                             mrow[:, g % 2, :]).then_inc(m_in[g % 2].sem, 16)

            def keep_residual(f, s):
                if h2_rdy.due(s, 0):
                    sp.wait_ge(h2_rdy.sem, h2_rdy.at(s, 0))
                sp.wait_ge(rows_in.sem, rows_in.at(f, 16 * T))
                sp.dma_start(res[f.parity][:, :, :], emb[f.parity][:, :, :]).then_inc(res_in.sem, 16)

            def start(s):
                f = s.plus(1)
                keep_residual(f, s)
                sp.dma_start(wo[:], w_o).then_inc(consts2.sem, 16)
                for part in range(3):
                    stack(sp, f, part, 0)
                max_rows(f, 0)
                sp.dma_start(we[:], w_exp).then_inc(experts_in.sem, 16)

            def pads(a, b):
                for e in range(a, b):
                    sp.dma_start(routed_rows[e * CAP:e * CAP + P, :].rearrange("p (a w) -> p a w", a=4),
                                 pad[:, :].unsqueeze(1).to_broadcast([P, 4, W // 4])).then_inc(padded.sem, 16)

            def body(s, first, last):
                f, b = s.plus(1), s.plus(-1)
                max_rows(s, 1)
                if last:
                    sp.wait_ge(pad_set.sem, 1)
                    pads(0, E // 2)
                if not last:
                    if s2_ps.due(s, 0):
                        sp.wait_ge(s2_ps.sem, s2_ps.at(s, 0))
                    stack(sp, f, 0, 0)
                    stack(sp, f, 1, 0)
                max_rows(s, 2)
                if last:
                    pads(E // 2, E + 1)
                if not last:
                    stack(sp, f, 0, 1)
                    stack(sp, f, 2, 0)
                    stack(sp, f, 1, 1)
                    stack(sp, f, 2, 1)
                    keep_residual(f, s)
                max_rows(s, 3)
                if not last:
                    max_rows(f, 0)
                if not first:
                    sp.wait_ge(routed.sem, routed.at(b, 16 * T))
                    sp.sem_inc(xr_free.sem, 1)

            schedule(sp, start, body, lambda s: None)

            def load(rd, u):
                row = sp.value_load(tiles[0:1, 0, bass.ds(tile_no(rd, u), 1)], min_val=0, max_val=E * CAP)
                if rd != (0, None):
                    sp.wait_ge(y_out[u].sem, value(y_out[u], rd, 0))
                sp.dma_start(xin[:, u, :], routed_rows[bass.ds(row, P), :]).then_inc(tile_in[u].sem, 16)

            sp.wait_ge(ta_step.sem, N_TA)
            sp.wait_ge(pv_done.sem, (B - 1) * pv_done.per)
            for n in range(NA):
                if n == VN // W:
                    sp.wait_ge(pv_done.sem, B * pv_done.per)
                load((n // RT, None), n % RT)
            sp.wait_ge(routed.sem, B * routed.per)
            sp.wait_ge(padded.sem, 16 * (E + 1))
            sp.wait_ge(tb_step.sem, N_TB)
            later_tiles(sp, load)
            for u in range(RT):
                sp.wait_ge(y_out[u].sem, NT // RT * 16)

        @block.gpsimd
        def _(pool):
            nc.gpsimd.memset(ids_all[:, B, :], DEPTH).then_inc(no_ids.sem, 1)
            for sig in (base, xr_free):
                pool.sem_inc(sig.sem, sig.primed)
            zero = pool.to_reg(0.0)
            pool.wait_ge(no_ids.sem, 1)
            pool.wait_ge(ids_in.sem, 16)

            def gather_start(n):
                if rows_in.due(n, 0):
                    pool.wait_ge(rows_in.sem, rows_in.at(n, 0))
                pool.sem_inc(waited.sem, 1)
                nc.gpsimd.tensor_copy(ids[:, :], ids_all[:, n.c, :] if n.q is None else
                                      ids_all[:, bass.ds(n.index, 1), :].rearrange("p a i -> p (a i)"))\
                    .then_inc(ids_cp.sem, 1)
                nc.gpsimd.memset(emb[n.parity][:, :, :], 0.0).then_inc(emb_zero.sem, 1)
                pool.wait_ge(ids_cp.sem, ids_cp.at(n, 1))
                pool.wait_ge(emb_zero.sem, emb_zero.at(n, 1))
                pool.sem_inc(waited.sem, 1)

            def gather(n, i):
                nc.gpsimd.indirect_dma_start(
                    out=emb[n.parity][:, i, :], out_offset=None, in_=weight,
                    in_offset=bass.IndirectOffsetOnAxis(ap=ids[:, i:i + 1].bitcast(U32), axis=0),
                    bounds_check=DEPTH - 1, oob_is_err=False).then_inc(rows_in.sem, 16)

            def rope_sum(f, t, eo):
                pool.wait_ge(turned.sem, turned.at(f, 4 * t + eo + 3))
                if t == 0:
                    if low.due(f, 0):
                        pool.wait_ge(low.sem, low.at(f, 0))
                nc.gpsimd.tensor_tensor(qk[:, t, eo, :], turn[:, 2 * eo, :], turn[:, 2 * eo + 1, :],
                                        ALU.add if eo else ALU.subtract).then_inc(roped.sem, 1)

            def rest(f, t):
                pool.wait_ge(high.sem, high.at(f, t + 1))
                nc.gpsimd.tensor_tensor(qk[:, t, :, :], qk[:, t, :, :], parts[:, 0, t, :, :],
                                        ALU.subtract).then_inc(less.sem, 1)

            def low_part(f, t):
                pool.wait_ge(middle.sem, middle.at(f, t + 1))
                nc.gpsimd.tensor_tensor(parts[:, 2, t, :, :], qk[:, t, :, :], parts[:, 1, t, :, :],
                                        ALU.subtract).then_inc(low.sem, 1)

            def mask_unit(s, g, k):
                n = g * N2 + k
                pool.wait_ge(exped.sem, exped.at(s, n + 1))
                pool.sem_inc(waited.sem, 1)
                v = p_unit(n, U2[k])[:, :, 0:P]
                nc.gpsimd.affine_select(out=v, in_=v, compare_op=ALU.is_ge, fill=zero, base=0,
                                        pattern=[[0, U2[k][2]], [1, P]],
                                        channel_multiplier=-1).then_inc(masked.sem, 1)

            def base_tile(k, i):
                pool.wait_ge(xn2_rdy.sem, xn2_rdy.at(k, i + 1))
                nc.gpsimd.tensor_tensor(xr[:, i, D:2 * D], h2[:, i, :], xn2[:, i, :],
                                        ALU.add).then_inc(base.sem, 1)

            def route(k, i):
                if i == 0:
                    pool.wait_ge(p_rdy.sem, p_rdy.at(k, 1))
                    pool.wait_ge(base.sem, base.at(k, T))
                    pool.sem_inc(waited.sem, 1)
                nc.gpsimd.indirect_dma_start(
                    out=routed_rows, in_=xr[:, i, :], in_offset=None,
                    out_offset=bass.IndirectOffsetOnAxis(ap=pos[:, 1, i:i + 1].bitcast(U32), axis=0),
                    bounds_check=E * CAP - 1, oob_is_err=False).then_inc(routed.sem, 16)

            def start(s):
                f, n = s.plus(1), s.plus(2)
                for m in (f, n):
                    gather_start(m)
                    for i in range(T):
                        gather(m, i)

            def body(s, first, last):
                f, b, n = s.plus(1), s.plus(-1), s.plus(2)
                for t in range(A2):
                    mask_unit(s, t // N2, t % N2)
                    if not last:
                        if t == 0:
                            pool.wait_ge(res_in.sem, res_in.at(s, 16))
                            gather_start(n)
                        if 1 <= t < 1 + T:
                            gather(n, t - 1)
                        if t in (6, 7):
                            rope_sum(f, 0, t - 6)
                        if t == 9:
                            rest(f, 0)
                        if t in (13, 14):
                            rope_sum(f, 1, t - 13)
                        if t == 15:
                            low_part(f, 0)
                        if t == 17:
                            rest(f, 1)
                        if t == 21:
                            low_part(f, 1)
                    if not first:
                        if 33 <= t < 33 + T:
                            base_tile(b, t - 33)
                        if t in (41, 42) and not last:
                            route(b, t - 41)
                        if t == 43:
                            for i in range(0 if last else 2, T):
                                route(b, i)

            def scatter(rd, u):
                pool.wait_ge(y_rdy.sem, value(y_rdy, rd, u + 1))
                pool.sem_inc(waited.sem, 1)
                nc.gpsimd.indirect_dma_start(
                    out=out_rows, in_=y[:, u, :], in_offset=None,
                    out_offset=bass.IndirectOffsetOnAxis(ap=xin[:, u, 2 * D:2 * D + 1].bitcast(U32), axis=0),
                    bounds_check=B * S - 1, oob_is_err=False).then_inc(y_out[u].sem, 16)

            def scatters(a, b):
                for n in range(a, b):
                    scatter((n // RT, None), n % RT)

            def end(s):
                scatters(0, 5)
                for i in range(T):
                    base_tile(s, i)
                scatters(5, 8)
                for i in range(T):
                    route(s, i)
                scatters(8, NA)

            schedule(pool, start, body, end)
            later_tiles(pool, scatter)

        @block.scalar
        def _(act):
            def copy(dst, src, done):
                nc.scalar.activation(dst, src, ACT.Copy).then_inc(done.sem, 1)

            def xT(n, c):
                act.wait_ge(xt_ps.sem, xt_ps.at(n, c + 1))
                if v_ps.due(n, 0):
                    act.wait_ge(v_ps.sem, v_ps.at(n, 0))
                copy(xnT[:, c, :], ps[:, misc(23 + 2 * c), :], xt_rdy)

            def v_half(s, k):
                f = s.plus(1)
                act.wait_ge(v_ps.sem, v_ps.at(f, k + 1))
                if pv_done.due(s, 0):
                    act.wait_ge(pv_done.sem, pv_done.at(s, 0))
                copy(vaug[f.parity][:, 2 * k:2 * k + 2, :, 0:HEAD_DIM],
                     ps[:, misc(12 + 3 * k), :].rearrange("p (i h d) -> p i h d", i=2, d=HEAD_DIM), v_rdy)

            def high_part(f, t):
                act.wait_ge(roped.sem, roped.at(f, 2 * t + 2))
                if stacked.due(f, 0):
                    act.wait_ge(stacked.sem, stacked.at(f, 0))
                copy(parts[:, 0, t, :, :], qk[:, t, :, :], high)

            def middle_part(f, t):
                act.wait_ge(less.sem, less.at(f, t + 1))
                copy(parts[:, 1, t, :, :], qk[:, t, :, :], middle)

            def max_row(s, g, bank):
                act.wait_ge(mt_ps.sem, mt_ps.at(s, g + 1))
                used = m_in[g % 2]
                if used.due(s, 16 * (g // 2)):
                    act.wait_ge(used.sem, used.at(s, 16 * (g // 2)))
                copy(mrow[:, g % 2, :], ps[0:MROWS * GROUP, bank, 0:S // 2].bitcast(BF16), mt_rdy)

            def exp_unit(s, g, k):
                n = g * N2 + k
                j, _, nh = U2[k]
                w = nh * (T - j) * P
                act.wait_ge(s2_ps.sem, s2_ps.at(s, n + 1))
                last_use = n - RING + 1 if n >= RING else n + (A2 - 1 - n) // RING * RING + 1 - A2
                if pv_done.due(s, last_use):
                    act.wait_ge(pv_done.sem, pv_done.at(s, last_use))
                nc.scalar.activation(probs[:, n % RING, 0:w], ps[:, S2B + n % 2, 0:w], ACT.Exp,
                                     scale=HEAD_DIM ** -0.5).then_inc(exped.sem, 1)

            def out_T(s, g):
                act.wait_ge(pv_done.sem, pv_done.at(s, (g + 1) * N2))
                if o_ps.due(s, g - 1):
                    act.wait_ge(o_ps.sem, o_ps.at(s, g - 1))
                copy(oT[:, g % 2, :], ps[:, PVB, :], ot_rdy)

            def attn_T(s, c):
                k = s.plus(-1)
                act.wait_ge(aT_ps.sem, aT_ps.at(k, c + 1))
                if g_ps.due(k, 0):
                    act.wait_ge(g_ps.sem, g_ps.at(k, 0))
                copy(bT[:, c, :], ps[:, misc(6 + c), :], aT_rdy)

            def x2_T(s, c):
                k = s.plus(-1)
                act.wait_ge(x2_ps.sem, x2_ps.at(k, c + 1))
                act.wait_ge(wo_ps.sem, wo_ps.at(k, 2))
                copy(bT[:, c, :], ps[:, misc(16 + c), :], x2_rdy)

            def start(s):
                f, n = s.plus(1), s.plus(2)
                xT(f, 0)
                xT(f, 1)
                act.wait_ge(s_init.sem, N_INIT)
                for t in range(2):
                    high_part(f, t)
                for t in range(2):
                    middle_part(f, t)
                for part in range(3):
                    stack(act, f, part, 1)
                v_half(s, 0)
                v_half(s, 1)
                max_row(f, 0, misc(19))
                xT(n, 0)
                xT(n, 1)

            def body(s, first, last):
                f, n = s.plus(1), s.plus(2)
                for t in range(A2):
                    g, k = t // N2, t % N2
                    exp_unit(s, g, k)
                    if k == 3 and not (first and g == 0):
                        out_T(s if g else s.plus(-1), (g - 1) % G)
                    if k == 5 and g < G - 1:
                        max_row(s, g + 1, misc((2, 8, 13)[g]))
                    if not last:
                        if t == 9:
                            high_part(f, 0)
                        if t == 12:
                            middle_part(f, 0)
                        if t == 16:
                            high_part(f, 1)
                        if t == 20:
                            middle_part(f, 1)
                        if t in (26, 31):
                            v_half(s, t // 31)
                        if t == 38:
                            max_row(f, 0, misc(19))
                        if t in (42, 43):
                            xT(n, t - 42)
                    if not first:
                        if t in (13, 15):
                            attn_T(s, t // 15)
                        if t in (34, 35):
                            x2_T(s, t - 34)

            def tile_T(rd, u):
                act.wait_ge(xi_ps.sem, value(xi_ps, rd, u + 1))
                act.wait_ge(y_ps.sem, value(y_ps, rd, u - 1))
                copy(xinT[:, u % 2, :, :].rearrange("p c n -> p (c n)"), ps[:, u % 2, 0:D], xi_rdy)

            def tiles_T(a, b):
                for n in range(a, b):
                    tile_T((n // RT, None), n % RT)

            def end(s):
                e = s.plus(1)
                out_T(s, G - 1)
                attn_T(e, 0)
                attn_T(e, 1)
                tiles_T(0, 6)
                x2_T(e, 0)
                x2_T(e, 1)
                tiles_T(6, NA)

            schedule(act, start, body, end)
            later_tiles(act, tile_T)

        @block.vector
        def _(dve):
            for p in range(2):
                nc.vector.memset(vaug[p], 1.0).then_inc(s_init.sem, 1)
            nc.vector.memset(pad[:, :], 1.0).then_inc(pad_set.sem, 1)
            for sig in (n_step[1], r_step, h2_rdy, y_rdy):
                dve.sem_inc(sig.sem, sig.primed)

            def norm(which, s, src, dst, ready, piece):
                step, st, agg, v = n_step[which], stats[:, which], mv[:, which], nv[:, which]
                done = [0, 1, 2, 3, 4, 8, 9, 10, 13, 16, 19][piece]

                def link(ins):
                    ins.then_inc(step.sem, 1)

                if piece < T:
                    link(nc.vector.bn_stats(st[:, piece, :], src[:, piece, :]))
                elif piece == 4:
                    dve.wait_ge(step.sem, step.at(s, done))
                    dve.sem_inc(waited.sem, 1)
                    for i in range(T):
                        link(nc.vector.bn_aggr(agg[:, i, :], st[:, i, :]))
                elif piece == 5:
                    dve.wait_ge(step.sem, step.at(s, done))
                    link(nc.vector.tensor_scalar(v[:, 0, :], agg[:, :, 1], EPS, None, ALU.add))
                elif piece == 6:
                    dve.wait_ge(step.sem, step.at(s, done))
                    link(nc.vector.tensor_scalar(v[:, 2, :].bitcast(I32), v[:, 0, :].bitcast(I32), -0.5,
                                                 float(0x5F3759DF), ALU.mult, ALU.add))
                elif piece < 10:
                    dve.wait_ge(step.sem, step.at(s, done))
                    link(nc.vector.tensor_tensor(v[:, 1, :], v[:, 2, :], v[:, 2, :], ALU.mult))
                    dve.wait_ge(step.sem, step.at(s, done + 1))
                    link(nc.vector.scalar_tensor_tensor(out=v[:, 3, :], in0=v[:, 1, :], scalar=-0.5,
                                                        in1=v[:, 0, :], op0=ALU.mult, op1=ALU.mult))
                    dve.wait_ge(step.sem, step.at(s, done + 2))
                    link(nc.vector.scalar_tensor_tensor(out=v[:, 2, :], in0=v[:, 3, :], scalar=1.5,
                                                        in1=v[:, 2, :], op0=ALU.add, op1=ALU.mult))
                else:
                    assert done == step.per
                    dve.wait_ge(step.sem, step.at(s, done))
                    for i in range(T):
                        nc.vector.tensor_scalar(dst[:, i, :], src[:, i, :], agg[:, i, 0:1], v[:, 2, i:i + 1],
                                                ALU.subtract, ALU.mult).then_inc(ready.sem, 1)

            def front_norm(f, piece):
                if piece == 0:
                    dve.wait_ge(rows_in.sem, rows_in.at(f, 16 * T))
                if piece == 10:
                    if xt_ps.due(f, 0):
                        dve.wait_ge(xt_ps.sem, xt_ps.at(f, 0))
                norm(0, f, emb[f.parity], xn, xn_rdy, piece)

            def back_norm(k, piece):
                if piece < T:
                    dve.wait_ge(h2_rdy.sem, h2_rdy.at(k, piece // 2 + 1))
                if piece == 10:
                    if xr_free.due(k, 0):
                        dve.wait_ge(xr_free.sem, xr_free.at(k, 0))
                norm(1, k, h2, xn2, xn2_rdy, piece)

            def products(f, t, x_):
                dve.wait_ge(qk_ps.sem, qk_ps.at(f, 2 * t + x_ + 1))
                if roped.due(f, 2 * t):
                    dve.wait_ge(roped.sem, roped.at(f, 2 * t))
                for eo in range(2):
                    nc.vector.tensor_tensor(turn[:, 2 * eo + x_, :], ps[:, misc(4 * t + x_), :],
                                            trig[:, (eo + x_) % 2, :], ALU.mult).then_inc(turned.sem, 1)

            def maximum(s, g, k):
                i, h0, n = U1[k]
                at = g * N1 + k
                dve.wait_ge(s1_ps.sem, s1_ps.at(s, at + 1))
                nc.vector.tensor_reduce(
                    negm[:, g % 2, i, h0:h0 + n],
                    ps[:, S1B + at % 3, 0:n * (i + 1) * P].rearrange("p (h w) -> p h w", h=n),
                    AX.X, ALU.max, negate=True).then_inc(s1_max.sem, 1)

            def split_max(s, g):
                dve.wait_ge(s1_max.sem, s1_max.at(s, (g + 1) * N1))
                if mt_ps.due(s, g - 1):
                    dve.wait_ge(mt_ps.sem, mt_ps.at(s, g - 1))
                m, r, q = negm[:, g % 2, :, :], mrest[:, g % 2, :, :], mparts[:, g % 2, :, :, :]
                nc.vector.tensor_copy(q[:, :, 0, :], m).then_inc(m_step.sem, 1)
                dve.wait_ge(m_step.sem, m_step.at(s, 3 * g + 1))
                nc.vector.tensor_tensor(r, m, q[:, :, 0, :], ALU.subtract).then_inc(m_step.sem, 1)
                dve.wait_ge(m_step.sem, m_step.at(s, 3 * g + 2))
                nc.vector.tensor_copy(q[:, :, 1, :], r).then_inc(m_step.sem, 1)
                dve.wait_ge(m_step.sem, m_step.at(s, 3 * g + 3))
                nc.vector.tensor_tensor(q[:, :, 2, :], r, q[:, :, 1, :], ALU.subtract).then_inc(m_rdy.sem, 1)

            def divide(s, g, bank):
                dve.wait_ge(o_ps.sem, o_ps.at(s, g + 1))
                o = ps[:, bank, :].rearrange("p (n d) -> p n d", d=2 * HEAD_DIM)
                r = rden[:, g % 2, :]
                nc.vector.reciprocal(r, o[:, :, HEAD_DIM]).then_inc(rd_rdy.sem, 1)
                dve.wait_ge(rd_rdy.sem, rd_rdy.at(s, g + 1))
                if g == 0:
                    if aT_ps.due(s, 0):
                        dve.wait_ge(aT_ps.sem, aT_ps.at(s, 0))
                w = GROUP * HEAD_DIM
                nc.vector.tensor_tensor(
                    attn[:, :, g * w:(g + 1) * w].rearrange("p i (h d) -> p i h d", d=HEAD_DIM),
                    ps[:, bank, :].rearrange("p (i h d) -> p i h d", i=T, d=2 * HEAD_DIM)[:, :, :, 0:HEAD_DIM],
                    r.rearrange("p (i h a) -> p i h a", i=T, a=1).to_broadcast([P, T, GROUP, HEAD_DIM]),
                    ALU.mult).then_inc(at_rdy.sem, 1)

            def residual(s, half):
                k = s.plus(-1)
                dve.wait_ge(wo_ps.sem, wo_ps.at(k, half + 1))
                dve.wait_ge(res_in.sem, res_in.at(k, 16))
                if base.due(k, 0):
                    dve.wait_ge(base.sem, base.at(k, 0))
                nc.vector.tensor_tensor(h2[:, 2 * half:2 * half + 2, :], res[k.parity][:, 2 * half:2 * half + 2, :],
                                        ps[:, misc(10 + half), :].rearrange("p (i d) -> p i d", i=2),
                                        ALU.add).then_inc(h2_rdy.sem, 1)

            def over(v):
                return v.unsqueeze(2).to_broadcast([P, T, E])

            def choose(s):
                k = s.plus(-1)
                dve.wait_ge(g_ps.sem, g_ps.at(k, 1))
                sc = ps[:, misc(18), 0:T * E].rearrange("p (i e) -> p i e", e=E)
                nc.vector.tensor_reduce(gmax[:, 0, :], sc, AX.X, ALU.max).then_inc(g_step.sem, 1)
                dve.wait_ge(g_step.sem, g_step.at(k, 1))
                nc.vector.tensor_tensor(gate[:, 0, :, :], sc, over(gmax[:, 0, :]), ALU.is_equal)\
                    .then_inc(g_step.sem, 1)
                dve.wait_ge(g_step.sem, g_step.at(k, 2))
                nc.vector.tensor_tensor(gate[:, 1, :, :], gate[:, 0, :, :],
                                        rank[:, :].unsqueeze(1).to_broadcast([P, T, E]), ALU.mult)\
                    .then_inc(g_step.sem, 1)
                dve.wait_ge(g_step.sem, g_step.at(k, 3))
                nc.vector.tensor_reduce(gmax[:, 1, :], gate[:, 1, :, :], AX.X, ALU.max)\
                    .then_inc(g_step.sem, 1)
                dve.wait_ge(g_step.sem, g_step.at(k, 4))
                nc.vector.tensor_tensor(onehot[:, :, :], gate[:, 1, :, :], over(gmax[:, 1, :]),
                                        ALU.is_equal).then_inc(g_step.sem, 1)

            def positions(s):
                k = s.plus(-1)
                nc.vector.tensor_copy(xr[:, :, 2 * D:W].bitcast(I32),
                                      tok[:, :].unsqueeze(2).to_broadcast([P, T, W - 2 * D]))\
                    .then_inc(r_step.sem, 1)
                dve.wait_ge(r_ps.sem, r_ps.at(k, 1))
                bank = misc(18)
                rk = ps[:, bank, T * E:2 * T * E].rearrange("p (i e) -> p i e", e=E)
                nc.vector.tensor_tensor(slot[:, 0, :, :], rk, cnt[:, :].unsqueeze(1).to_broadcast([P, T, E]),
                                        ALU.add).then_inc(r_step.sem, 1)
                dve.wait_ge(r_step.sem, r_step.at(k, 2))
                nc.vector.tensor_tensor(cnt[:, :], cnt[:, :], ps[:, bank, 2 * T * E:2 * T * E + E], ALU.add)\
                    .then_inc(r_step.sem, 1)
                nc.vector.tensor_scalar(tok[:, :], tok[:, :], float(S), None, ALU.add).then_inc(r_step.sem, 1)
                nc.vector.tensor_tensor(slot[:, 1, :, :], slot[:, 0, :, :], onehot[:, :, :], ALU.mult)\
                    .then_inc(r_step.sem, 1)
                dve.wait_ge(r_step.sem, r_step.at(k, 5))
                nc.vector.tensor_reduce(pos[:, 0, :], slot[:, 1, :, :], AX.X, ALU.add).then_inc(r_step.sem, 1)
                dve.wait_ge(r_step.sem, r_step.at(k, 6))
                nc.vector.tensor_copy(pos[:, 1, :].bitcast(I32), pos[:, 0, :]).then_inc(p_rdy.sem, 1)

            def ahead(s, t):
                n = t + LEAD
                return (s if n < A1 else s.plus(1)), n // N1 % G, n % N1

            def start(s):
                f, n = s.plus(1), s.plus(2)
                for piece in range(11):
                    front_norm(f, piece)
                dve.wait_ge(consts.sem, 16 * N_CONST)
                for t in range(2):
                    products(f, t, 0)
                    products(f, t, 1)
                    for eo in range(2):
                        dve.wait_ge(turned.sem, turned.at(f, 4 * t + eo + 3))
                        nc.vector.tensor_tensor(qk[:, t, eo, :], turn[:, 2 * eo, :], turn[:, 2 * eo + 1, :],
                                                ALU.add if eo else ALU.subtract).then_inc(roped.sem, 1)
                for t in range(2):
                    dve.wait_ge(high.sem, high.at(f, t + 1))
                    nc.vector.tensor_tensor(qk[:, t, :, :], qk[:, t, :, :], parts[:, 0, t, :, :],
                                            ALU.subtract).then_inc(less.sem, 1)
                for t in range(2):
                    dve.wait_ge(middle.sem, middle.at(f, t + 1))
                    nc.vector.tensor_tensor(parts[:, 2, t, :, :], qk[:, t, :, :], parts[:, 1, t, :, :],
                                            ALU.subtract).then_inc(low.sem, 1)
                dve.wait_ge(consts2.sem, 16 * N_CONST2)
                for piece in range(11):
                    front_norm(n, piece)
                for t in range(A1 - LEAD, A1):
                    maximum(*ahead(s, t))
                    if t == A1 - LEAD + N1 - 1:
                        split_max(f, 0)

            def body(s, first, last):
                f, b, n = s.plus(1), s.plus(-1), s.plus(2)
                for t in range(A1):
                    if not last or t + LEAD < A1:
                        maximum(*ahead(s, t))
                    if t % N1 == 3 and not (last and t // N1 == G - 1):
                        split_max(*ahead(s, t)[0:2])
                    if not last:
                        if t in (1, 4):
                            products(f, 0, t // 4)
                        if t in (9, 12):
                            products(f, 1, t // 12)
                        for piece in {16: (0,), 17: (1,), 18: (2, 3), 20: (4, 5), 22: (6, 7), 23: (8,),
                                      33: (9,), 34: (10,)}.get(t, ()):
                            front_norm(n, piece)
                    if not first:
                        if t == 7:
                            divide(b, G - 1, misc(3))
                        if t in (20, 23):
                            residual(s, t // 23)
                        for piece in {21: (0,), 22: (1,), 24: (2, 3), 26: (4, 5), 27: (6, 7), 28: (8,), 30: (9,),
                                      31: (10,)}.get(t, ()):
                            back_norm(b, piece)
                        if t == 37:
                            choose(s)
                        if t == 39:
                            positions(s)
                    if t in (18, 29, 40):
                        divide(s, t // N1 - 1, misc((9, 14, 21)[t // N1 - 1]))

            k = [0]

            def cut(at, n):
                return tab[:, at:at + n]

            starts = cut(0, E)
            fills = cut(E, 32)
            fills1 = cut(E + 32, 32)
            below = cut(E + 64, E * E).rearrange("p (e f) -> p e f", f=E)
            number = cut(E + 64 + E * E, NT)
            first_row = cut(E + 64 + E * E + NT, NT)
            counts, per, ends = tn[:, 0, 0:E], tn[:, 1, 0:E], tn[:, 2, 0:E]
            begun, ended, hop = tn[:, 3, 0:E], tn[:, 4, 0:E], tn[:, 5, 0:E]
            expert, row = tn[:, 6, :], tn[:, 7, :]

            def step(sig, ins):
                ins.then_inc(sig.sem, 1)
                k[0] += 1
                dve.wait_ge(sig.sem, k[0])

            def tile_counts(sig, limits, op):
                step(sig, nc.vector.tensor_tensor(counts, cnt[0:1, :], starts, ALU.subtract))
                f = tw[:, 0, 0:E * 32].rearrange("p (e k) -> p e k", k=32)
                step(sig, nc.vector.tensor_tensor(f, counts.unsqueeze(2).to_broadcast([1, E, 32]),
                                                  limits.unsqueeze(1).to_broadcast([1, E, 32]), op))
                step(sig, nc.vector.tensor_reduce(per, f, AX.X, ALU.add))

            def tile_ends(sig):
                t = tw[:, 1, 0:E * E].rearrange("p (e f) -> p e f", f=E)
                step(sig, nc.vector.tensor_tensor(t, below, per.unsqueeze(1).to_broadcast([1, E, E]), ALU.mult))
                step(sig, nc.vector.tensor_reduce(ends, t, AX.X, ALU.add))

            def tile_experts(sig, n):
                o = tw[:, 2, 0:n * E].rearrange("p (j e) -> p j e", e=E)
                step(sig, nc.vector.tensor_tensor(o, ends.unsqueeze(1).to_broadcast([1, n, E]),
                                                  number[:, 0:n].unsqueeze(2).to_broadcast([1, n, E]), ALU.is_le))
                step(sig, nc.vector.tensor_reduce(expert[:, 0:n], o, AX.X, ALU.add))

            def tile_hops(sig, n):
                o = tw[:, 2, 0:n * E].rearrange("p (j e) -> p j e", e=E)
                w = tw[:, 3, 0:n * E].rearrange("p (j e) -> p j e", e=E)
                step(sig, nc.vector.tensor_tensor(w, o, hop.unsqueeze(1).to_broadcast([1, n, E]), ALU.mult))
                step(sig, nc.vector.tensor_reduce(row[:, 0:n], w, AX.X, ALU.add))

            def first_tiles():
                sig = ta_step
                tile_counts(sig, fills1, ALU.is_ge)
                tile_ends(sig)
                tile_experts(sig, NA)
                step(sig, nc.vector.tensor_scalar(hop, per, float(-P), float(CAP), ALU.mult, ALU.add))
                tile_hops(sig, NA)
                step(sig, nc.vector.tensor_tensor(tiles[:, 0, 0:NA], row[:, 0:NA], first_row[:, 0:NA], ALU.add))
                step(sig, nc.vector.tensor_copy(tiles[:, 1, 0:NA], expert[:, 0:NA]))
                step(sig, nc.vector.tensor_tensor(begun, ends, per, ALU.subtract))
                step(sig, nc.vector.tensor_scalar(begun, begun, float(NA), None, ALU.min))
                step(sig, nc.vector.tensor_scalar(ended, ends, float(NA), None, ALU.min))
                step(sig, nc.vector.tensor_tensor(done[:, :], ended, begun, ALU.subtract))
                step(sig, nc.vector.memset(shift[:, E:E + 1], float(2 * E * CAP)))
                assert k[0] == N_TA
                k[0] = 0

            def later_tile_counts():
                sig = tb_step
                tile_counts(sig, fills, ALU.is_gt)
                step(sig, nc.vector.tensor_tensor(per, per, done[:, :], ALU.subtract))
                tile_ends(sig)

            def later_tile_rows():
                sig, n = tb_step, NT - NA
                tile_experts(sig, n)
                step(sig, nc.vector.scalar_tensor_tensor(out=shift[:, 0:E], in0=ends, scalar=float(-P),
                                                         in1=cnt[0:1, :], op0=ALU.mult, op1=ALU.add))
                step(sig, nc.vector.tensor_tensor(hop, shift[:, 1:E + 1], shift[:, 0:E], ALU.subtract))
                tile_hops(sig, n)
                step(sig, nc.vector.tensor_tensor(row[:, 0:n], row[:, 0:n], first_row[:, 0:n], ALU.add))
                step(sig, nc.vector.tensor_tensor(row[:, 0:n], row[:, 0:n], shift[:, 0:1].to_broadcast([1, n]),
                                                  ALU.add))
                step(sig, nc.vector.tensor_scalar(tiles[:, 0, NA:NT], row[:, 0:n], float(-P), float(E * CAP),
                                                  ALU.add, ALU.min))
                step(sig, nc.vector.tensor_scalar(tiles[:, 1, NA:NT], expert[:, 0:n], float(E - 1), None, ALU.min))
                assert k[0] == N_TB, k

            def tile_sum(rd, u):
                dve.wait_ge(y_ps.sem, value(y_ps, rd, u + 1))
                nc.vector.tensor_tensor(y[:, u, :], ps[:, YB[u % 2], 0:D], xin[:, u, D:2 * D],
                                        ALU.add).then_inc(y_rdy.sem, 1)

            def tile_sums(a, b):
                for n in range(a, b):
                    tile_sum((n // RT, None), n % RT)

            def end(s):
                e = s.plus(1)
                first_tiles()
                divide(s, G - 1, misc(3))
                residual(e, 0)
                residual(e, 1)
                for piece in range(11):
                    back_norm(s, piece)
                    if 5 <= piece < 10:
                        tile_sums(piece - 5, piece - 4)
                tile_sums(5, 6)
                choose(e)
                tile_sums(6, 8)
                positions(e)
                later_tile_counts()
                tile_sums(8, 10)
                later_tile_rows()
                tile_sums(10, NA)

            schedule(dve, start, body, end)
            later_tiles(dve, tile_sum)

        @block.tensor
        def _(pe):
            for sig in (aT_ps, g_ps, y_ps):
                pe.sem_inc(sig.sem, sig.primed)
            pe.wait_ge(consts.sem, 16 * N_CONST)

            def turn_rows(src, bank, c, done):
                for i in range(T):
                    mm = pe.transpose(ps[:, bank, i * P:(i + 1) * P], src[:, i, c * P:(c + 1) * P], idf[:, :])
                mm.then_inc(done.sem, 1)

            def turn_xn(n, c):
                pe.wait_ge(xn_rdy.sem, xn_rdy.at(n, T))
                turn_rows(xn, misc(23 + 2 * c), c, xt_ps)

            def project_qk(f, n, c):
                mm = pe.matmul(ps[:, misc((0, 1, 4, 5)[n]), :], wqk[:, c, n, :], xnT[:, c, :],
                               start=(c == 0), stop=(c == C - 1))
                if c == C - 1:
                    mm.then_inc(qk_ps.sem, 1)

            def tokens_by(src, w, bank, tile, done):
                for c in range(C):
                    mm = pe.matmul(ps[:, bank, tile % 2 * D:(tile % 2 + 1) * D], src[:, c, tile * P:(tile + 1) * P],
                                   w[:, c, :], start=(c == 0), stop=(c == C - 1))
                if tile % 2:
                    mm.then_inc(done.sem, 1)

            def turn_max(s, g, bank):
                pe.wait_ge(m_rdy.sem, m_rdy.at(s, g + 1))
                view = ps[0:MROWS * GROUP, bank, 0:S // 2].bitcast(BF16)
                for i in range(T):
                    mm = pe.transpose(view[:, i * P:(i + 1) * P],
                                      mparts[:, g % 2, i, :, :].rearrange("p a h -> p (a h)"), idb[:, :])
                mm.then_inc(mt_ps.sem, 1)

            def turn_out(s, g, bank):
                pe.wait_ge(ot_rdy.sem, ot_rdy.at(s, g + 1))
                for i in range(T):
                    mm = pe.transpose(ps[:, bank, i * P:(i + 1) * P], oT[:, g % 2, i * P:(i + 1) * P], idf[:, :])
                mm.then_inc(o_ps.sem, 1)

            def pass1_unit(s, g, k):
                i, h0, n = U1[k]
                at = g * N1 + k
                w = (i + 1) * P
                bank = S1B + at % 3
                if at == 0:
                    pe.wait_ge(stacked.sem, stacked.at(s, stacked.per))
                read = at - 2 if at >= 3 else (-1, 0, -2)[at]
                if s1_max.due(s, read):
                    pe.wait_ge(s1_max.sem, s1_max.at(s, read))
                q, kk = qs[s.parity], ks[s.parity]
                for x_ in range(n):
                    hd = g * GROUP + h0 + x_
                    pe.matmul(ps[:, bank, x_ * w:(x_ + 1) * w], q[0:TROWS, hd, i * P:(i + 1) * P],
                              kk[0:TROWS, hd, 0:w], start=True, stop=False)
                    mm = pe.matmul(ps[:, bank, (x_ + 1) * w - P:(x_ + 1) * w], idb[:, :],
                                   causal[:, :], start=False, stop=True)
                mm.then_inc(s1_ps.sem, 1)

            def pass2_unit(s, g, k):
                j, h0, n = U2[k]
                at = g * N2 + k
                w = (T - j) * P
                if k == 0:
                    pe.wait_ge(m_in[g % 2].sem, m_in[g % 2].at(s, 16 * (g // 2 + 1)))
                if exped.due(s, at - 1):
                    pe.wait_ge(exped.sem, exped.at(s, at - 1))
                for x_ in range(n):
                    hd = g * GROUP + h0 + x_
                    mm = pe.matmul(ps[:, S2B + at % 2, x_ * w:(x_ + 1) * w],
                                   ks[s.parity][:, hd, j * P:(j + 1) * P], qs[s.parity][:, hd, j * P:S],
                                   start=True, stop=True)
                mm.then_inc(s2_ps.sem, 1)

            def pv(s, g, j):
                if j == 0:
                    if ot_rdy.due(s, g):
                        pe.wait_ge(ot_rdy.sem, ot_rdy.at(s, g))
                    pe.wait_ge(v_rdy.sem, v_rdy.at(s, 2))
                units = [k for k, u in enumerate(U2) if u[0] == j]
                pe.wait_ge(masked.sem, masked.at(s, g * N2 + units[-1] + 1))
                for k in units:
                    _, h0, nh = U2[k]
                    pr = p_unit(g * N2 + k, U2[k])
                    for x_ in range(nh):
                        hh = h0 + x_
                        mm = pe.matmul(ps[32 * hh:32 * hh + 32, PVB, j * P:S],
                                       vaug[s.parity][:, j, g * GROUP + hh, :], pr[:, x_, :],
                                       start=(j == 0), stop=(j == T - 1))
                    mm.then_inc(pv_done.sem, 1)

            def gates(s):
                k = s.plus(-1)
                pe.wait_ge(x2_rdy.sem, x2_rdy.at(k, C))
                for i in range(T):
                    for c in range(C):
                        mm = pe.matmul(ps[:, misc(18), i * E:(i + 1) * E], bT[:, c, i * P:(i + 1) * P],
                                       wg[:, c, :], start=(c == 0), stop=(c == C - 1))
                mm.then_inc(g_ps.sem, 1)

            def ranks(s):
                pe.wait_ge(g_step.sem, g_step.at(s.plus(-1), g_step.per))
                for i in range(T + 1):
                    for j in range(min(i + 1, T)):
                        mm = pe.matmul(ps[:, misc(18), (T + i) * E:(T + i + 1) * E],
                                       before[:, 0 if i == j else 1, :], onehot[:, j, :],
                                       start=(j == 0), stop=(j == min(i, T - 1)))
                mm.then_inc(r_ps.sem, 1)

            def ahead(s, t):
                n = t + LEAD
                return (s if n < A1 else s.plus(1)), n // N1 % G, n % N1

            def start(s):
                f, n = s.plus(1), s.plus(2)
                turn_xn(f, 0)
                pe.wait_ge(xt_rdy.sem, xt_rdy.at(f, 1))
                turn_xn(f, 1)
                pe.wait_ge(xt_rdy.sem, xt_rdy.at(f, C))
                for c in range(C):
                    project_qk(f, 0, c)
                for c in range(C):
                    project_qk(f, 1, c)
                pe.wait_ge(turned.sem, turned.at(f, 2))
                for c in range(C):
                    project_qk(f, 2, c)
                pe.wait_ge(turned.sem, turned.at(f, 4))
                for c in range(C):
                    project_qk(f, 3, c)
                pe.wait_ge(turned.sem, turned.at(f, 6))
                tokens_by(xnT, wv, misc(12), 0, v_ps)
                tokens_by(xnT, wv, misc(12), 1, v_ps)
                pe.wait_ge(turned.sem, turned.at(f, 8))
                tokens_by(xnT, wv, misc(15), 2, v_ps)
                tokens_by(xnT, wv, misc(15), 3, v_ps)
                pe.wait_ge(s_init.sem, N_INIT)
                pe.wait_ge(consts2.sem, 16 * N_CONST2)
                for t in range(A1 - LEAD, A1):
                    pass1_unit(*ahead(s, t))
                    if t == A1 - 5:
                        pe.wait_ge(v_rdy.sem, v_rdy.at(f, 2))
                        turn_max(f, 0, misc(19))
                pe.wait_ge(mt_rdy.sem, mt_rdy.at(f, 1))
                turn_xn(n, 0)
                pe.wait_ge(xt_rdy.sem, xt_rdy.at(n, 1))
                turn_xn(n, 1)

            def body(s, first, last):
                f, b, n = s.plus(1), s.plus(-1), s.plus(2)
                for t in range(A2):
                    g, k = t // N2, t % N2
                    pass2_unit(s, g, k)
                    if k in (2, 3) and not (first and g == 0):
                        pv(s if g else b, (g - 1) % G, k)
                    if not last or t + LEAD < A1:
                        pass1_unit(*ahead(s, t))
                    if k == 6:
                        pv(s, g, 0)
                    if k == 10:
                        pv(s, g, 1)
                    if t == 0 and not last:
                        if first:
                            pe.wait_ge(v_rdy.sem, v_rdy.at(s, 1))
                        else:
                            pe.wait_ge(r_step.sem, r_step.at(b, 0))
                        pe.wait_ge(xt_rdy.sem, xt_rdy.at(f, 1))
                        project_qk(f, 0, 0)
                    if t == 1 and not last:
                        pe.wait_ge(xt_rdy.sem, xt_rdy.at(f, 2))
                        project_qk(f, 0, 1)
                    if t in (2, 4) and not last:
                        project_qk(f, 1, t // 4)
                    if t == 5:
                        if not last:
                            pe.wait_ge(turned.sem, turned.at(f, 2))
                        else:
                            pe.wait_ge(r_step.sem, r_step.at(b, 0))
                        turn_max(s, 1, misc(2))
                    if t == 7 and not first:
                        if not last:
                            pe.wait_ge(turned.sem, turned.at(f, 4))
                        else:
                            pe.wait_ge(xt_rdy.sem, xt_rdy.at(f, 2))
                        turn_out(b, G - 1, misc(3))
                    if t in (8, 9) and not last:
                        pe.wait_ge(mt_rdy.sem, mt_rdy.at(s, 2))
                        project_qk(f, 2, t - 8)
                    if t in (11, 12) and not last:
                        if first:
                            pe.wait_ge(turned.sem, turned.at(f, 4))
                        else:
                            pe.wait_ge(at_rdy.sem, at_rdy.at(b, G))
                        project_qk(f, 3, t - 11)
                    if t == 13 and not first:
                        pe.wait_ge(at_rdy.sem, at_rdy.at(b, G))
                        if not last:
                            pe.wait_ge(turned.sem, turned.at(f, 6))
                        else:
                            pe.wait_ge(mt_rdy.sem, mt_rdy.at(s, 2))
                        turn_rows(attn, misc(6), 0, aT_ps)
                    if t == 15 and not first:
                        if not last:
                            pe.wait_ge(turned.sem, turned.at(f, 8))
                        turn_rows(attn, misc(7), 1, aT_ps)
                    if t == 16:
                        if first:
                            pe.wait_ge(turned.sem, turned.at(f, 6))
                        else:
                            pe.wait_ge(aT_rdy.sem, aT_rdy.at(b, 1))
                        turn_max(s, 2, misc(8))
                    if t == 18:
                        if first:
                            pe.wait_ge(turned.sem, turned.at(f, 8))
                        else:
                            pe.wait_ge(aT_rdy.sem, aT_rdy.at(b, 2))
                        turn_out(s, 0, misc(9))
                    if t in (19, 20) and not first:
                        pe.wait_ge(aT_rdy.sem, aT_rdy.at(b, C))
                        pe.wait_ge(mt_rdy.sem, mt_rdy.at(s, 3))
                        tokens_by(bT, wo, misc(10), t - 19, wo_ps)
                    if t in (22, 23) and not first:
                        pe.wait_ge(at_rdy.sem, at_rdy.at(s, 1))
                        tokens_by(bT, wo, misc(11), t - 20, wo_ps)
                    if t in (25, 26) and not last:
                        if first:
                            pe.wait_ge(mt_rdy.sem, mt_rdy.at(s, 3))
                        else:
                            pe.wait_ge(h2_rdy.sem, h2_rdy.at(b, 1))
                        tokens_by(xnT, wv, misc(12), t - 25, v_ps)
                    if t == 27:
                        if first:
                            pe.wait_ge(at_rdy.sem, at_rdy.at(s, 1))
                        else:
                            pe.wait_ge(h2_rdy.sem, h2_rdy.at(b, 2))
                        turn_max(s, 3, misc(13))
                    if t == 29:
                        if last:
                            pe.wait_ge(h2_rdy.sem, h2_rdy.at(b, 1))
                        else:
                            pe.wait_ge(v_rdy.sem, v_rdy.at(f, 1))
                        turn_out(s, 1, misc(14))
                    if t in (30, 31) and not last:
                        pe.wait_ge(mt_rdy.sem, mt_rdy.at(s, 4))
                        tokens_by(xnT, wv, misc(15), t - 28, v_ps)
                    if t == 34 and not first:
                        pe.wait_ge(xn2_rdy.sem, xn2_rdy.at(b, T))
                        pe.wait_ge(at_rdy.sem, at_rdy.at(s, 2))
                        turn_rows(xn2, misc(16), 0, x2_ps)
                    if t == 35 and not first:
                        if last:
                            pe.wait_ge(mt_rdy.sem, mt_rdy.at(s, 4))
                        else:
                            pe.wait_ge(v_rdy.sem, v_rdy.at(f, 2))
                        turn_rows(xn2, misc(17), 1, x2_ps)
                    if t == 37 and not first:
                        gates(s)
                    if t == 38 and not last:
                        if first:
                            pe.wait_ge(v_rdy.sem, v_rdy.at(f, 2))
                        else:
                            pe.wait_ge(x2_rdy.sem, x2_rdy.at(b, 2))
                        turn_max(f, 0, misc(19))
                    if t == 39 and not first:
                        ranks(s)
                    if t == 40:
                        if not last:
                            pe.wait_ge(mt_rdy.sem, mt_rdy.at(f, 1))
                        else:
                            pe.wait_ge(x2_rdy.sem, x2_rdy.at(b, 2))
                        turn_out(s, 2, misc(21))
                    if t == 42 and not last:
                        pe.wait_ge(at_rdy.sem, at_rdy.at(s, 3))
                        turn_xn(n, 0)
                    if t == 43 and not last:
                        pe.wait_ge(xt_rdy.sem, xt_rdy.at(n, 1))
                        turn_xn(n, 1)

            def turn_tile(rd, u):
                pe.wait_ge(tile_in[u].sem, value(tile_in[u], rd, 16))
                for c in range(C):
                    mm = pe.transpose(ps[:, u % 2, c * P:(c + 1) * P], xin[:, u, c * P:(c + 1) * P], idf[:, :])
                mm.then_inc(xi_ps.sem, 1)

            def expert_tile(rd, u):
                e = pe.value_load(tiles[0:1, 1, bass.ds(tile_no(rd, u), 1)], min_val=0, max_val=E - 1)
                pe.wait_ge(xi_rdy.sem, value(xi_rdy, rd, u + 1))
                pe.wait_ge(y_rdy.sem, value(y_rdy, rd, u - 1))
                for c in range(C):
                    mm = pe.matmul(ps[:, YB[u % 2], 0:D], xinT[:, u % 2, c, :],
                                   we[:, c, bass.ds(e, 1), :].rearrange("p a d -> p (a d)"),
                                   start=(c == 0), stop=(c == C - 1))
                mm.then_inc(y_ps.sem, 1)

            def expert_tiles(a, b):
                for n in range(a, b):
                    if n + 1 < NA:
                        turn_tile(((n + 1) // RT, None), (n + 1) % RT)
                    expert_tile((n // RT, None), n % RT)

            def end(s):
                e = s.plus(1)
                pv(s, G - 1, 2)
                pv(s, G - 1, 3)
                pe.wait_ge(at_rdy.sem, at_rdy.at(s, 3))
                turn_out(s, G - 1, misc(3))
                pe.wait_ge(at_rdy.sem, at_rdy.at(s, G))
                pe.wait_ge(r_step.sem, r_step.at(s, 0))
                turn_rows(attn, misc(6), 0, aT_ps)
                turn_rows(attn, misc(7), 1, aT_ps)
                pe.wait_ge(aT_rdy.sem, aT_rdy.at(s, C))
                for tile in range(T):
                    tokens_by(bT, wo, misc(10 + tile // 2), tile, wo_ps)
                pe.wait_ge(ta_step.sem, N_TA)
                pe.wait_ge(experts_in.sem, 16)
                turn_tile((0, None), 0)
                expert_tiles(0, 5)
                pe.wait_ge(xn2_rdy.sem, xn2_rdy.at(s, T))
                for c in range(C):
                    turn_rows(xn2, misc(16 + c), c, x2_ps)
                expert_tiles(5, 6)
                gates(e)
                expert_tiles(6, 8)
                ranks(e)
                expert_tiles(8, NA)

            schedule(pe, start, body, end)

            pe.wait_ge(tb_step.sem, N_TB)

            def later_tile(rd, u):
                if u == 0 or (rd, u) == ((NA // RT, None), NA % RT):
                    turn_tile(rd, u)
                if u + 1 < RT:
                    turn_tile(rd, u + 1)
                expert_tile(rd, u)

            later_tiles(pe, later_tile)


def kernel(x, L0_tok_weight, L0_attn_W_qkv, L0_attn_W_o, L0_ffn_gate_w, L0_ffn_expert_w):
    import ml_dtypes
    import concourse.bacc as bacc
    from concourse.bass_utils import run_bass_kernel_spmd

    D = L0_tok_weight.shape[1]
    B, S = x.shape
    E = L0_ffn_gate_w.shape[0]
    C = D // P

    def chunks(w_t):
        return np.ascontiguousarray(w_t.reshape(C, P, -1).transpose(1, 0, 2))

    wqkv = np.asarray(L0_attn_W_qkv)
    w_qk = np.stack([wqkv[t * D:(t + 1) * D].reshape(HEADS, PAIRS, 2, D)[:, :, eo].transpose(1, 0, 2).reshape(P, D)
                     for t in range(2) for eo in range(2)])
    w_qk = np.ascontiguousarray(w_qk.transpose(2, 0, 1).reshape(C, P, 4, P).transpose(1, 0, 2, 3))
    w_exp = np.asarray(L0_ffn_expert_w).transpose(2, 0, 1).reshape(C, P, E, D).transpose(1, 0, 2, 3)

    inv = np.float32(ROPE_THETA) ** (np.arange(0, HEAD_DIM, 2, dtype=np.float32) / np.float32(HEAD_DIM))
    ang = np.arange(S, dtype=np.float32)[None, :] / inv[:, None].astype(np.float32)
    cos, sin = (np.repeat(f(ang).astype(np.float32), HEADS, axis=0) for f in (np.cos, np.sin))
    rope = np.stack([cos, sin], axis=1)
    ident = np.eye(P, dtype=np.float32)
    upper = np.triu(np.full((P, P), NEG, np.float32), 1).astype(ml_dtypes.bfloat16)
    cap = P + B * S
    nt = B * S // P + E
    before = np.stack([np.triu(np.ones((P, P)), 1), np.ones((P, P))], axis=1).astype(ml_dtypes.bfloat16)
    cnt = np.tile(np.arange(E, dtype=np.float32) * cap + P, (P, 1))
    tok = np.ascontiguousarray(np.arange(S, dtype=np.float32).reshape(S // P, P).T)
    tab = np.concatenate([np.arange(E) * cap + P, np.arange(32) * P, np.arange(1, 33) * P,
                          np.tril(np.ones((E, E))).ravel(),
                          np.arange(nt), np.arange(1, nt + 1) * P])[None].astype(np.float32)
    rank = np.tile(np.arange(E, 0, -1, dtype=np.float32), (P, 1))

    arrays = {
        "x": np.ascontiguousarray(np.asarray(x).reshape(B, S // P, P).transpose(2, 0, 1)),
        "weight": np.ascontiguousarray(L0_tok_weight),
        "w_qk": w_qk, "w_v": chunks(wqkv[2 * D:].T), "w_o": chunks(np.asarray(L0_attn_W_o).T),
        "w_gate": chunks(np.asarray(L0_ffn_gate_w).T), "w_exp": np.ascontiguousarray(w_exp),
        "rope": rope, "ident": ident, "identb": ident.astype(ml_dtypes.bfloat16), "mask": upper, "rank": rank,
        "before": before, "cnt": cnt, "tok": tok, "tab": tab,
        "ones": np.ones((MROWS, HEADS, S), ml_dtypes.bfloat16),
    }
    nc = bacc.Bacc("TRN2", target_bir_lowering=False, num_devices=1)
    t = {n: nc.dram_tensor(f"in_{n}", a.shape, mybir.dt.from_np(a.dtype), kind="ExternalInput").ap()
         for n, a in arrays.items()}
    out = nc.dram_tensor("out", (B, S, D), F32, kind="ExternalOutput").ap()
    tower(nc, t["x"], t["weight"], t["w_qk"], t["w_v"], t["w_o"], t["w_gate"], t["w_exp"], t["rope"],
          t["ident"], t["identb"], (t["mask"], t["rank"]), (t["before"], t["cnt"], t["tok"], t["tab"], t["ones"]), out)
    r = run_bass_kernel_spmd(nc, [{f"in_{n}": a for n, a in arrays.items()}], core_ids=[0])
    return r.results[0]["out"]
```
